# Optimizing a Trainium2 kernel written in Bass

```python
import numpy as np
import jax
import jax.numpy as jnp

def _softmax(x, axis=-1):
    return jax.nn.softmax(x, axis=axis)

def _gelu(x):
    return jax.nn.gelu(x, approximate=True)

def _silu(x):
    return jax.nn.silu(x)

def _sigmoid(x):
    return jax.nn.sigmoid(x)

def _layernorm(x, axis=-1, eps=1e-05):
    m = jnp.mean(x, axis=axis, keepdims=True)
    v = jnp.var(x, axis=axis, keepdims=True)
    return (x - m) / jnp.sqrt(v + eps)

def _scatter_add(tgt, idx, src, axis=0):
    return tgt.at[idx].add(src)

def _segment_sum(src, seg, n):
    return jax.ops.segment_sum(src, seg, n)
kernel_name = 'mk_decoder_postln_d1_seqx_r8_edfbc4'

def setup_inputs(seed: int=0):
    np.random.seed(seed)
    _w = jnp.asarray

    def _rec_inputs():
        import jax
        import jax.numpy as jnp
        _rk = jax.random.key(seed)
        x = -0.0002928 + 1 * jax.random.normal(jax.random.fold_in(_rk, 1), (2, 256, 128), jnp.float32)
        _lenS = 256 - jax.random.randint(jax.random.fold_in(_rk, 7), (2,), 0, max(1, 256 // 4) + 1, jnp.int32)
        _lenS2 = 512 - jax.random.randint(jax.random.fold_in(_rk, 8), (2,), 0, max(1, 512 // 4) + 1, jnp.int32)
        _ctx_1024P = jax.random.normal(jax.random.fold_in(_rk, 11), (2, 16, 128), jnp.float32)
        _ctx_1024c = jax.random.dirichlet(jax.random.fold_in(_rk, 511), 0.3 * jnp.ones((16,), jnp.float32), (2, 512))
        _ctx_1024t = jnp.einsum('bsk,bkd->bsd', _ctx_1024c, _ctx_1024P)
        _ctx_1024t = _ctx_1024t * jax.lax.rsqrt(jnp.mean(jnp.square(_ctx_1024t)) + 1e-12) * 0.953939
        ctx_1024 = -1.39393e-06 + 0.999914 * (_ctx_1024t + 0.3 * jax.random.normal(jax.random.fold_in(_rk, 611), (2, 512, 128), jnp.float32))
        _validS = jnp.arange(256)[None, :] < _lenS[:, None]
        _validS2 = jnp.arange(512)[None, :] < _lenS2[:, None]
        _causal = jnp.tril(jnp.ones((256, 256), dtype=bool))
        mask_1x1xSxS2_ik0 = jnp.where(jnp.broadcast_to(_validS2[0:1, None, None, :], (1, 1, 256, 512)), 0, 1).astype(jnp.int32)
        return (x, ctx_1024, mask_1x1xSxS2_ik0)
    x, ctx_1024, mask_1x1xSxS2_ik0 = _rec_inputs()

    def _L0_attn_setup():
        import jax, jax.numpy as jnp
        import numpy as np
        T, B, E = (128, 4, 128)
        H = 16
        D = E // H
        L = 16
        key = jax.random.key(seed)
        ks = jax.random.split(key, 4)
        query = jax.random.normal(ks[0], (T, B, E), dtype=jnp.float32)
        in_proj_weight = jax.random.normal(ks[1], (3 * E, E), dtype=jnp.float32) * (1.0 / np.sqrt(E))
        in_proj_bias = jnp.zeros((3 * E,), dtype=jnp.float32)
        rel_pos_keys = jax.random.normal(ks[2], (2 * L + 1, E), dtype=jnp.float32) * (1.0 / np.sqrt(E))
        out_w = jax.random.normal(ks[3], (E, E), dtype=jnp.float32) * (1.0 / np.sqrt(E))
        out_b = jnp.zeros((E,), dtype=jnp.float32)
        return {'query': query, 'in_proj_weight': in_proj_weight, 'in_proj_bias': in_proj_bias, 'rel_pos_keys': rel_pos_keys, 'out_w': out_w, 'out_b': out_b}
    _L0_attn_all = _L0_attn_setup()
    _L0_attn_in = {k: v for k, v in _L0_attn_all.items() if k in ('in_proj_weight', 'in_proj_bias', 'rel_pos_keys', 'out_w', 'out_b')}
    del _L0_attn_all

    def _L0_xattn_setup():
        import jax, jax.numpy as jnp
        import numpy as np
        import math
        B, S, D, H = (2, 256, 128, 16)
        DK = D // H

        def _split_heads(x):
            b, s, _ = x.shape
            return x.reshape(b, s, H, DK).transpose(0, 2, 1, 3)
        key = jax.random.key(seed)
        ks = jax.random.split(key, 12)
        std = 1.0 / math.sqrt(D)
        inp = {'q': jax.random.normal(ks[0], (B, S, D), jnp.float32), 'k': jax.random.normal(ks[1], (B, S, D), jnp.float32), 'v': jax.random.normal(ks[2], (B, S, D), jnp.float32), 'mask': jnp.tril(jnp.ones((S, S), jnp.int32))[None, None, :, :], 'wq': jax.random.normal(ks[3], (D, D), jnp.float32) * std, 'bq': jax.random.normal(ks[4], (D,), jnp.float32) * std, 'wk': jax.random.normal(ks[5], (D, D), jnp.float32) * std, 'bk': jax.random.normal(ks[6], (D,), jnp.float32) * std, 'wv': jax.random.normal(ks[7], (D, D), jnp.float32) * std, 'bv': jax.random.normal(ks[8], (D,), jnp.float32) * std, 'wo': jax.random.normal(ks[9], (D, D), jnp.float32) * std, 'bo': jax.random.normal(ks[10], (D,), jnp.float32) * std}
        return inp
    _L0_xattn_all = _L0_xattn_setup()
    _L0_xattn_in = {k: v for k, v in _L0_xattn_all.items() if k in ('wq', 'bq', 'wk', 'bk', 'wv', 'bv', 'wo', 'bo')}
    del _L0_xattn_all

    def _L0_ffn_setup():
        import jax, jax.numpy as jnp
        import numpy as np
        B, S, DIM = (4, 256, 128)
        E, K, HID = (8, 2, 512)
        key = jax.random.key(seed)
        ks = jax.random.split(key, 8)
        init = lambda k, sh: jax.random.normal(k, sh, jnp.float32) * 0.02
        return {'x': jax.random.normal(ks[0], (B, S, DIM), jnp.float32), 'gate_w': init(ks[1], (DIM, E)), 'gate_b': jnp.zeros((E,), jnp.float32), 'w1': init(ks[2], (E, DIM, HID)), 'b1': jnp.zeros((E, HID), jnp.float32), 'w2': init(ks[3], (E, HID, DIM)), 'b2': jnp.zeros((E, DIM), jnp.float32), 'ws1': init(ks[4], (DIM, HID)), 'bs1': jnp.zeros((HID,), jnp.float32), 'ws2': init(ks[5], (HID, DIM)), 'bs2': jnp.zeros((DIM,), jnp.float32)}
    _L0_ffn_all = _L0_ffn_setup()
    _L0_ffn_in = {k: v for k, v in _L0_ffn_all.items() if k in ('gate_w', 'gate_b', 'w1', 'b1', 'w2', 'b2', 'ws1', 'bs1', 'ws2', 'bs2')}
    del _L0_ffn_all
    return {'x': x, 'ctx_1024': ctx_1024, 'mask_1x1xSxS2_ik0': mask_1x1xSxS2_ik0, 'L0_attn_in_proj_weight': _L0_attn_in['in_proj_weight'], 'L0_attn_in_proj_bias': _L0_attn_in['in_proj_bias'], 'L0_attn_rel_pos_keys': _L0_attn_in['rel_pos_keys'], 'L0_attn_out_w': _L0_attn_in['out_w'], 'L0_attn_out_b': _L0_attn_in['out_b'], 'L0_xattn_wq': _L0_xattn_in['wq'], 'L0_xattn_bq': _L0_xattn_in['bq'], 'L0_xattn_wk': _L0_xattn_in['wk'], 'L0_xattn_bk': _L0_xattn_in['bk'], 'L0_xattn_wv': _L0_xattn_in['wv'], 'L0_xattn_bv': _L0_xattn_in['bv'], 'L0_xattn_wo': _L0_xattn_in['wo'], 'L0_xattn_bo': _L0_xattn_in['bo'], 'L0_ffn_gate_w': _L0_ffn_in['gate_w'], 'L0_ffn_gate_b': _L0_ffn_in['gate_b'], 'L0_ffn_w1': _L0_ffn_in['w1'], 'L0_ffn_b1': _L0_ffn_in['b1'], 'L0_ffn_w2': _L0_ffn_in['w2'], 'L0_ffn_b2': _L0_ffn_in['b2'], 'L0_ffn_ws1': _L0_ffn_in['ws1'], 'L0_ffn_bs1': _L0_ffn_in['bs1'], 'L0_ffn_ws2': _L0_ffn_in['ws2'], 'L0_ffn_bs2': _L0_ffn_in['bs2']}

def reference(x, ctx_1024, mask_1x1xSxS2_ik0, L0_attn_in_proj_weight, L0_attn_in_proj_bias, L0_attn_rel_pos_keys, L0_attn_out_w, L0_attn_out_b, L0_xattn_wq, L0_xattn_bq, L0_xattn_wk, L0_xattn_bk, L0_xattn_wv, L0_xattn_bv, L0_xattn_wo, L0_xattn_bo, L0_ffn_gate_w, L0_ffn_gate_b, L0_ffn_w1, L0_ffn_b1, L0_ffn_w2, L0_ffn_b2, L0_ffn_ws1, L0_ffn_bs1, L0_ffn_ws2, L0_ffn_bs2):
    import jax
    import jax.numpy as jnp

    def _L0_attn_ref(query, in_proj_weight, in_proj_bias, rel_pos_keys, out_w, out_b):
        import jax, jax.numpy as jnp
        import numpy as np
        T, B, E = (128, 4, 128)
        H = 16
        D = E // H
        L = 16
        t, b, e = query.shape
        scaling = D ** (-0.5)
        qkv = jnp.einsum('tbe,fe->tbf', query, in_proj_weight) + in_proj_bias
        q, k, v = jnp.split(qkv, 3, axis=-1)
        q = q * scaling

        def heads(x):
            return x.reshape(t, b * H, D).transpose(1, 0, 2)
        q, k, v = (heads(q), heads(k), heads(v))
        r = jnp.arange(t)
        dist = jnp.clip(r[None, :] - r[:, None], -L, L) + L
        rel_k = rel_pos_keys[dist][:, :, :D]
        scores = jnp.einsum('btd,bsd->bts', q, k) + jnp.einsum('btd,tsd->bts', q, rel_k)
        probs = jax.nn.softmax(scores, axis=-1)
        attn = jnp.einsum('bts,bsd->btd', probs, v)
        attn = attn.transpose(1, 0, 2).reshape(t, b, e)
        return jnp.einsum('tbe,oe->tbo', attn, out_w) + out_b

    def _L0_xattn_ref(q, k, v, mask, wq, bq, wk, bk, wv, bv, wo, bo):
        import jax, jax.numpy as jnp
        import numpy as np
        import math
        B, S, D, H = (2, 256, 128, 16)
        DK = D // H

        def _split_heads(x):
            b, s, _ = x.shape
            return x.reshape(b, s, H, DK).transpose(0, 2, 1, 3)
        query = _split_heads(q @ wq.T + bq)
        key_h = _split_heads(k @ wk.T + bk)
        value = _split_heads(v @ wv.T + bv)
        scale = 1.0 / math.sqrt(DK)
        scores = jnp.einsum('bhqd,bhkd->bhqk', query, key_h) * scale
        scores = jnp.where(mask == 0, jnp.float32(-1000000000.0), scores)
        attn = jax.nn.softmax(scores, axis=-1)
        x = jnp.einsum('bhqk,bhkd->bhqd', attn, value)
        x = x.transpose(0, 2, 1, 3).reshape(q.shape[0], -1, H * DK)
        return x @ wo.T + bo

    def _L0_ffn_ref(x, gate_w, gate_b, w1, b1, w2, b2, ws1, bs1, ws2, bs2):
        import jax, jax.numpy as jnp
        import numpy as np
        B, S, DIM = (4, 256, 128)
        E, K, HID = (8, 2, 512)
        orig_shape = x.shape
        xf = x.reshape(-1, DIM)
        logits = xf @ gate_w + gate_b
        top_w, top_i = jax.lax.top_k(logits, K)
        gw = jax.nn.softmax(top_w, axis=-1).astype(xf.dtype)
        combine = (gw[:, :, None] * jax.nn.one_hot(top_i, E, dtype=xf.dtype)).sum(axis=1)
        out = jnp.zeros_like(xf)
        for e in range(E):
            h = jax.nn.gelu(xf @ w1[e] + b1[e], approximate=False)
            out = out + combine[:, e:e + 1] * (h @ w2[e] + b2[e])
        shared = jax.nn.gelu(xf @ ws1 + bs1, approximate=False) @ ws2 + bs2
        return (out + shared).reshape(orig_shape)
    x = _layernorm(x + _L0_attn_ref(x, L0_attn_in_proj_weight, L0_attn_in_proj_bias, L0_attn_rel_pos_keys, L0_attn_out_w, L0_attn_out_b), axis=-1)
    x = _layernorm(x + _L0_xattn_ref(x, ctx_1024, ctx_1024, mask_1x1xSxS2_ik0, L0_xattn_wq, L0_xattn_bq, L0_xattn_wk, L0_xattn_bk, L0_xattn_wv, L0_xattn_bv, L0_xattn_wo, L0_xattn_bo), axis=-1)
    x = _layernorm(x + _L0_ffn_ref(x, L0_ffn_gate_w, L0_ffn_gate_b, L0_ffn_w1, L0_ffn_b1, L0_ffn_w2, L0_ffn_b2, L0_ffn_ws1, L0_ffn_bs1, L0_ffn_ws2, L0_ffn_bs2), axis=-1)
    return x

_drawn_inputs = setup_inputs


def setup_inputs(seed=0):
    import zlib

    import numpy as np

    out = dict(_drawn_inputs(seed))
    spreads = {'L0_attn_in_proj_bias': (0.0, 0.1),
     'L0_attn_out_b': (0.0, 0.1),
     'L0_ffn_gate_b': (0.0, 0.1),
     'L0_ffn_b1': (0.0, 0.489),
     'L0_ffn_b2': (0.0, 0.1),
     'L0_ffn_bs1': (0.0, 0.377),
     'L0_ffn_bs2': (0.0, 0.1)}
    factors = {'L0_xattn_bq': 3.068, 'L0_xattn_bk': 8.0}
    for name, (base, spread) in spreads.items():
        noise = np.random.default_rng([zlib.crc32(name.encode()), seed]).standard_normal(out[name].shape)
        drawn = base * np.exp(spread * noise) if base else spread * noise
        out[name] = jnp.asarray(drawn.astype(out[name].dtype))
    for name, factor in factors.items():
        out[name] = (out[name] * factor).astype(out[name].dtype)
    return out
```

```python
from contextlib import ExitStack

import concourse.bass as bass
from concourse import mybir

F32 = mybir.dt.float32
F32R = mybir.dt.float32r
BF16 = mybir.dt.bfloat16
I32 = mybir.dt.int32
U32 = mybir.dt.uint32
ALU = mybir.AluOpType
ACT = mybir.ActivationFunctionType
AX = mybir.AxisListType

P = 128
B = 2
S = 256
SK = 512
H = 16
D = P // H
NT = B * S // P
QT = S // P
KT = SK // P
E = 8
EX = E + 1
HID = 512
HC = HID // P
GH = 4
NG = H // GH
QROWS = 32
VROWS = 16
STEPS = B * NG
LN_EPS = 1e-5
HEAD_SCALE = float(D) ** -0.5
NEG = -1e9
LOWEST = -3.0e38
REL = 16

PROJ_W = 4 * P
ROW = {}
_at = 0
for _name, _n in (("in_b", 3 * P), ("rel", 3 * D), ("out_b", P), ("bq", P), ("bv", P), ("bo", P),
                  ("gate_b", E), ("iota", E), ("e", 4), ("minus_half", 4)):
    ROW[_name] = (_at, _at + _n)
    _at += _n
ROW_N = _at
COL = {}
_at = 0
for _name, _n in (("ident", P), ("out_w", P), ("wq", P), ("wo", P), ("gate_w", E), ("b1", EX * HC), ("bk", 1)):
    COL[_name] = (_at, _at + _n)
    _at += _n
COL_N = _at


def decoder_layer(nc, x_t_w, x_tok, ctx_w, cols, rows, b2_rows, mask, w1, w2, out):
    with ExitStack() as ctx:
        def sb(name, shape, dt=F32):
            return ctx.enter_context(nc.sbuf_tensor(name, shape, dt))

        def sem(name):
            return ctx.enter_context(nc.semaphore(name))

        def views(region, *shapes):
            out, at = [], 0
            for shape in shapes:
                n = 1
                for k in shape:
                    n *= k
                v = region[:, at:at + n]
                names = "abcd"[:len(shape)]
                if len(shape) > 1:
                    v = v.rearrange(f"p ({' '.join(names)}) -> p {' '.join(names)}", **dict(zip(names, shape)))
                out.append(v)
                at += n
            assert at <= region.shape[1]
            return out

        region_p = sb("region_p", [P, 2 * GH * KT * S])
        region_m = sb("region_m", [P, QT * SK + B * PROJ_W])
        region_n = sb("region_n", [P, QT * SK])
        region_x = sb("region_x", [P, B * S + PROJ_W])
        region_j = sb("region_j", [P, 4 * SK // 2])
        region_b = sb("region_b", [P, NT * P])
        region_t = sb("region_t", [P, NT * P])
        [xw] = views(region_x, (B * S + PROJ_W,))
        kf, kh_, kl_, cw, qkkv, prod, xtok = views(
            region_p, (B * SK,), (B * SK,), (B * SK,), (B * SK + 2 * P,),
            (NT, PROJ_W), (B, B, QT * P),
            (NT, P))
        kh, kl = kh_.bitcast(F32R), kl_.bitcast(F32R)
        col = sb("col", [P, COL_N])
        row = sb("row", [P, ROW_N])
        b2r = sb("b2r", [EX, P])
        msk, bias_qkkv = views(region_m, (QT, SK), (B, PROJ_W))
        msk = msk.bitcast(I32)
        w1s = sb("w1s", [P, EX, HID])
        w2s = sb("w2s", [P, EX, HC, P])

        def rw(name):
            return row[:, ROW[name][0]:ROW[name][1]]

        def cl(name):
            return col[:, COL[name][0]:COL[name][1]]

        ident = cl("ident")
        sc = sb("sc", [P, B, B, QT * H])
        smax = sb("smax", [P, B, QT * H])
        sd = sb("sd", [P, B, B, QT * H])
        se = sb("se", [P, B, B, QT * H])
        ssum = sb("ssum", [P, B, QT * H])
        srec = sb("srec", [P, B, QT * H])
        sp_ = sb("sp_", [P, B, B, QT * H])
        att, att_t = views(region_j, (NT, P), (NT * P,))
        [xb] = views(region_b, (NT, P))
        res = sb("res", [P, NT, P])
        stats = sb("stats", [P, NT, 6])
        mv = sb("mv", [P, NT, 2])
        vare = sb("vare", [P, NT])
        rstd = sb("rstd", [P, NT])
        x1 = sb("x1", [P, NT, P])
        [x1b] = views(region_b, (NT, P))
        [x1_t] = views(region_t, (NT * P,))
        [nz] = views(region_n, (QT, SK))
        any_ = sb("any_", [P, QT])
        qsc = sb("qsc", [P, QT])
        big = sb("big", [P, QT])
        bqs = sb("bqs", [P, QT, P])
        mbias = sb("mbias", [P, QT, SK])
        mbias_t = sb("mbias_t", [P, KT, S], BF16)
        ident_b = sb("ident_b", [P, P], BF16)
        kx = sb("kx", [P, NG, GH, B * SK], F32R)
        ones = sb("ones", [2, S])
        vx = sb("vx", [P, B * KT, H, VROWS])
        qf = sb("qf", [P, NT, P])
        qx = sb("qx", [P, NT, H, QROWS])
        qx_t = sb("qx_t", [P, NG, NT * P], F32R)
        qm_t = sb("qm_t", [P, 2, S], F32R)
        junk = region_j[:, :].bitcast(BF16).rearrange("p (n k) -> p n k", n=4)
        rowmax = sb("rowmax", [P, NT, H])
        [pt] = views(region_p, (2 * GH, KT * S))
        orec = sb("orec", [P, QT, GH])
        att2, ot = views(region_x, (NT, P), (2, S))
        [att2_t, comb_t] = views(region_t, (S,), (S,))
        x2, x2_t = views(region_n, (NT, P), (B, S))
        logit = sb("logit", [P, NT, E])
        top = sb("top", [P, NT, 8])
        topi = sb("topi", [P, NT, 8], U32)
        topf = sb("topf", [P, NT, 2])
        gap = sb("gap", [P, NT])
        e2 = sb("e2", [P, NT])
        den = sb("den", [P, NT])
        gw = sb("gw", [P, NT, 2])
        hot = sb("hot", [P, NT, E])
        comb = sb("comb", [P, NT, EX])
        hs, acc, fin = views(region_m, (4, S), (NT, P), (NT, P))

        bank = [ctx.enter_context(nc.psum_tensor(f"bank{i}", [P, 512], F32)) for i in range(8)]
        turn = bank[7]

        in_row, in_xw, in_cw, in_col = sem("in_row"), sem("in_xw"), sem("in_cw"), sem("in_col")
        in_x, in_mask, in_w1, in_w2, in_b2 = sem("in_x"), sem("in_mask"), sem("in_w1"), sem("in_w2"), sem("in_b2")
        in_ones, ones_ready, kx_rows, out_done = sem("in_ones"), sem("ones_ready"), sem("kx_rows"), sem("out_done")
        qkv_ready, qkv_taken = sem("qkv_ready"), sem("qkv_taken")
        sd_ready, se_ready = sem("sd_ready"), sem("se_ready")
        att_ready = sem("att_ready")
        var_ready, rstd_ready = sem("var_ready"), sem("rstd_ready")
        x1_ready, xb_ready = sem("x1_ready"), sem("xb_ready")
        kt_ready, kt_taken = sem("kt_ready"), sem("kt_taken")
        v_ready, v_taken = sem("v_ready"), sem("v_taken")
        kx_zero_v, kx_zero_g, kx_zero_a, vx_pad = sem("kx_zero_v"), sem("kx_zero_g"), sem("kx_zero_a"), sem("vx_pad")
        kl_ready, identb_ready = sem("kl_ready"), sem("identb_ready")
        mbias_ready, mt_ready, mt_taken = sem("mbias_ready"), sem("mt_ready"), sem("mt_taken")
        qx_ready, qxt_ready, qxt_taken = sem("qx_ready"), sem("qxt_ready"), sem("qxt_taken")
        turn_full, turn_free = sem("turn_full"), sem("turn_free")
        s_ready, max_done, negmax_ready = sem("s_ready"), sem("max_done"), sem("negmax_ready")
        st_ready, exp_done = sem("st_ready"), sem("exp_done")
        pv_ready, pv_taken, pv_zero = sem("pv_ready"), sem("pv_taken"), sem("pv_zero")
        att2_ready, x2_ready, comb_ready = sem("att2_ready"), sem("x2_ready"), sem("comb_ready")
        gap_ready, e2_ready = sem("gap_ready"), sem("e2_ready")
        up_ready, gelu_done, down_done, acc_done = sem("up_ready"), sem("gelu_done"), sem("down_done"), sem("acc_done")
        fin_ready = sem("fin_ready")
        v_chain, g_chain = sem("v_chain"), sem("g_chain")

        turns = []
        for what in ("att_t0", "att_t1", "out_w0", "out_w1", "x1_t0", "x1_t1", "q0", "q1"):
            turns.append(what)
        for i in range(STEPS):
            turns.append(f"qm{i}")
            if i >= 2:
                turns.append(f"o{i - 2}")
            if i == 6:
                turns += ["att2_t0", "wo0"]
            if i == 7:
                turns += ["x2_t0", "gate0"]
        turns += ["o6", "comb_t0", "o7", "b20", "att2_t1", "wo1", "x2_t1", "gate1", "comb_t1", "b21"]
        turn_no = {what: k for k, what in enumerate(turns)}

        def full(what):
            return turn_no[what] + 1

        UNITS = B * EX * HC
        block = ctx.enter_context(nc.Block())

        @block.sync
        def _(sp):
            sp.dma_start(xw[:, :], x_t_w).then_inc(in_xw, 16)
            sp.dma_start(cw[:, :], ctx_w).then_inc(in_cw, 16)
            sp.dma_start(col[:, :], cols).then_inc(in_col, 16)
            sp.dma_start(xtok[:, :, :], x_tok).then_inc(in_x, 16)
            sp.dma_start(msk[:, :, :], mask).then_inc(in_mask, 16)
            sp.wait_ge(ones_ready, 1)
            sp.wait_ge(kx_zero_v, 1)
            sp.wait_ge(kx_zero_a, 1)
            sp.wait_ge(kx_zero_g, 1)
            for g in range(GH):
                for a in range(NG):
                    sp.dma_start(kx[32 * g:32 * g + 2, a, g, :].rearrange("p (r n) -> p r n", n=S).bitcast(F32),
                                 ones[0:2, :].unsqueeze(1).broadcast_to([2, B * SK // S, S])).then_inc(in_ones, 16)
            sp.wait_ge(kt_taken, 4)
            for j, part in ((0, kh_), (2, kh_), (1, kl_)):
                if j == 1:
                    sp.wait_ge(kl_ready, 1)
                for a in range(NG):
                    for g in range(GH):
                        h = GH * a + g
                        r = 32 * g + 2 + D * j
                        sp.dma_start(kx[r:r + D, a, g, :].bitcast(F32), part[D * h:D * h + D, :]).then_inc(kx_rows, 16)
            sp.dma_start(w1s[:, :, :], w1).then_inc(in_w1, 16)
            sp.dma_start(b2r[:, :], b2_rows).then_inc(in_b2, 16)
            sp.dma_start(w2s[:, :, :, :], w2).then_inc(in_w2, 16)
            for b in range(B):
                sp.wait_ge(fin_ready, b + 1)
                sp.dma_start(out[b].rearrange("(t p) d -> p t d", p=P), fin[:, 2 * b:2 * b + 2, :])\
                    .then_inc(out_done, 16)
            sp.wait_ge(out_done, 16 * B)

        @block.gpsimd
        def _(pool):
            pool.memset(ones[:, :], 1.0).then_inc(ones_ready, 1)
            pool.memset(kx[:, 2:4, :, :].bitcast(F32), 0.0).then_inc(kx_zero_g, 1)
            pool.wait_ge(kt_taken, 4)
            pool.tensor_tensor(kl[:, :], kf[:, :], kh[:, :].bitcast(F32), ALU.subtract).then_inc(kl_ready, 1)
            pool.memset(vx[:, :, :, D:D + 1], 1.0).then_inc(vx_pad, 1)
            pool.memset(vx[:, :, :, D + 1:VROWS], 0.0).then_inc(vx_pad, 1)

            def inv_sqrt(k, t0):
                pool.wait_ge(var_ready, k)
                pool.tensor_tensor(rstd[:, t0:t0 + 2], vare[:, t0:t0 + 2], rw("minus_half")[:, 0:2], ALU.pow)\
                    .then_inc(rstd_ready, 1)

            def router_exp(b):
                pool.wait_ge(gap_ready, b + 1)
                pool.tensor_tensor(e2[:, 2 * b:2 * b + 2], rw("e")[:, 0:2], gap[:, 2 * b:2 * b + 2], ALU.pow)\
                    .then_inc(e2_ready, 1)

            inv_sqrt(1, 0)
            inv_sqrt(2, 2)
            inv_sqrt(3, 0)
            router_exp(0)
            inv_sqrt(4, 2)
            router_exp(1)
            inv_sqrt(5, 0)
            inv_sqrt(6, 2)

        @block.scalar
        def _(act):
            act.dma_start(row[:, :], rows).then_inc(in_row, 16)

            act.wait_ge(kx_zero_v, 1)
            act.activation(kx[:, 1, :, :], kx[:, 0, :, :].bitcast(F32), ACT.Copy).then_inc(kx_zero_a, 1)
            act.wait_ge(in_col, 16)
            for b in range(B):
                act.wait_ge(kt_ready, b + 1)
                act.activation(kf[:, b * SK:(b + 1) * SK], bank[4 + b][:, :], ACT.Identity, bias=cl("bk"))\
                    .then_inc(kt_taken, 1)
                act.activation(kh[:, b * SK:(b + 1) * SK], bank[4 + b][:, :], ACT.Identity, bias=cl("bk"))\
                    .then_inc(kt_taken, 1)
            act.wait_ge(sd_ready, 1)
            act.activation(se[:, :, :, :], sd[:, :, :, :], ACT.Exp, scale=HEAD_SCALE).then_inc(se_ready, 1)
            for half in range(2):
                act.wait_ge(mt_ready, half + 1)
                act.activation(mbias_t[:, 2 * half:2 * half + 2, :].rearrange("p k q -> p (k q)"),
                               bank[half][:, :], ACT.Copy).then_inc(mt_taken, 1)

            def take(what, dst, src):
                act.wait_ge(turn_full, full(what))
                act.activation(dst, src, ACT.Copy).then_inc(turn_free, 1)

            for b in range(B):
                take(f"att_t{b}", att_t[:, b * S:(b + 1) * S], turn[:, 0:S])
            for b in range(B):
                take(f"x1_t{b}", x1_t[:, b * S:(b + 1) * S], turn[:, 0:S])
            for k in range(4):
                act.wait_ge(qxt_ready, k + 1)
                b, pair = k // 2, k % 2
                act.activation(qx_t[:, 2 * pair:2 * pair + 2, b * S:(b + 1) * S],
                               bank[2 + k][:, :].rearrange("p (a q) -> p a q", a=2), ACT.Copy).then_inc(qxt_taken, 1)

            for i in range(STEPS):
                if i >= 2:
                    act.wait_ge(st_ready, GH * (i - 1))
                take(f"qm{i}", qm_t[:, i % 2, :], turn[:, 0:S])
                for g in range(GH):
                    n = GH * i + g
                    act.wait_ge(st_ready, n + 1)
                    if i >= 2:
                        act.wait_ge(pv_ready, i - 1)
                    pair = 2 + 2 * (n % 2)
                    for j in range(2):
                        act.activation(pt[:, n % (2 * GH), 512 * j:512 * j + 512], bank[pair + j][:, :], ACT.Exp)\
                            .then_inc(exp_done, 1)
                    if g == 1 and i >= 1:
                        if i >= 3:
                            act.wait_ge(turn_full, full(f"o{i - 3}"))
                        act.wait_ge(pv_ready, i)
                        act.activation(ot[:, (i - 1) % 2, :], bank[6][:, 0:S], ACT.Copy).then_inc(pv_taken, 1)
                    if i == 6 and g == 3:
                        take("att2_t0", att2_t[:, :], turn[:, 0:S])
                if i == 7:
                    take("x2_t0", x2_t[:, 0, :], turn[:, 0:S])
            act.wait_ge(turn_full, full("o5"))
            act.wait_ge(pv_ready, STEPS)
            act.activation(ot[:, (STEPS - 1) % 2, :], bank[6][:, 0:S], ACT.Copy).then_inc(pv_taken, 1)
            for u in range(UNITS):
                b, e, hc = u // (EX * HC), u // HC % EX, u % HC
                act.wait_ge(up_ready, u + 1)
                if u >= 4:
                    act.wait_ge(down_done, u - 3)
                act.activation(hs[:, u % 4, :], bank[u % 4][:, 0:S], ACT.Gelu,
                               bias=col[:, COL["b1"][0] + e * HC + hc:COL["b1"][0] + e * HC + hc + 1])\
                    .then_inc(gelu_done, 1)
                if u == 1:
                    take("comb_t0", comb_t[0:EX, :], turn[0:EX, 0:S])
                if u == 7:
                    take("att2_t1", att2_t[:, :], turn[:, 0:S])
                if u == 15:
                    take("x2_t1", x2_t[:, 1, :], turn[:, 0:S])
                if u == 25:
                    take("comb_t1", comb_t[0:EX, :], turn[0:EX, 0:S])

        @block.tensor
        def _(pe):
            def turn_begin(what):
                if turn_no[what]:
                    pe.wait_ge(turn_free, turn_no[what])

            pe.wait_ge(in_xw, 16)
            for t in range(NT):
                pe.matmul(bank[t][:, :], xw[:, t * P:(t + 1) * P], xw[:, B * S:B * S + PROJ_W],
                          start=True, stop=True).then_inc(qkv_ready, 1)
            pe.wait_ge(in_cw, 16)
            for b in range(B):
                pe.matmul(bank[4 + b][:, :], cw[:, B * SK:B * SK + P], cw[:, b * SK:(b + 1) * SK],
                          start=True, stop=True).then_inc(kt_ready, 1)
            for b in range(B):
                for k in range(KT):
                    mm = pe.matmul(bank[6 + b][:, k * P:(k + 1) * P], cw[:, (b * KT + k) * P:(b * KT + k + 1) * P],
                                   cw[:, B * SK + P:B * SK + 2 * P], start=True, stop=True)
                mm.then_inc(v_ready, 1)
            pe.wait_ge(in_col, 16)
            pe.wait_ge(mbias_ready, QT)
            for half in range(2):
                pe.wait_ge(qkv_taken, half + 1)
                for k in range(2):
                    for q in range(QT):
                        kt = 2 * half + k
                        mm = pe.transpose(bank[half][:, (k * QT + q) * P:(k * QT + q + 1) * P],
                                          mbias[:, q, kt * P:(kt + 1) * P], ident)
                mm.then_inc(mt_ready, 1)

            def turn_tiles(what, src, b):
                turn_begin(what)
                for q in range(QT):
                    mm = pe.transpose(turn[:, q * P:(q + 1) * P], src[:, 2 * b + q, :], ident)
                mm.then_inc(turn_full, 1)

            def turn_product(what, lhs, rhs, n):
                turn_begin(what)
                for q in range(QT):
                    mm = pe.matmul(turn[:, q * P:q * P + n], lhs[:, q * P:(q + 1) * P], rhs, start=True, stop=True)
                mm.then_inc(turn_full, 1)

            pe.wait_ge(v_taken, 2)
            for b in range(B):
                pe.wait_ge(att_ready, b + 1)
                turn_tiles(f"att_t{b}", att, b)
            for b in range(B):
                pe.wait_ge(turn_free, full(f"att_t{b}"))
                turn_product(f"out_w{b}", att_t[:, b * S:(b + 1) * S], cl("out_w"), P)
            for b in range(B):
                pe.wait_ge(x1_ready, b + 1)
                turn_tiles(f"x1_t{b}", x1, b)
            for b in range(B):
                pe.wait_ge(turn_free, full(f"x1_t{b}"))
                turn_product(f"q{b}", x1_t[:, b * S:(b + 1) * S], cl("wq"), P)
            pe.wait_ge(qkv_taken, NT)
            pe.wait_ge(kt_taken, 4)
            for k in range(4):
                b, pair = k // 2, k % 2
                pe.wait_ge(qx_ready, b + 1)
                for a2 in range(2):
                    a = 2 * pair + a2
                    for q in range(QT):
                        mm = pe.transpose(bank[2 + k][:, (a2 * QT + q) * P:(a2 * QT + q + 1) * P],
                                          qx[:, 2 * b + q, GH * a:GH * a + GH, :], ident)
                mm.then_inc(qxt_ready, 1)

            def scores(i, g):
                b, a = i // NG, i % NG
                for q in range(QT):
                    n = 2 * (GH * i + g) + q
                    if n >= 2:
                        pe.wait_ge(max_done, n - 1)
                    pe.matmul(bank[n % 2][:, :], qx_t[:, a, (2 * b + q) * P:(2 * b + q + 1) * P],
                              kx[:, a, g, b * SK:(b + 1) * SK], start=True, stop=True).then_inc(s_ready, 1)

            def turn_negmax(i):
                b, a = i // NG, i % NG
                pe.wait_ge(negmax_ready, i + 1)
                turn_begin(f"qm{i}")
                for q in range(QT):
                    mm = pe.transpose(turn[:, q * P:(q + 1) * P], qx[:, 2 * b + q, GH * a:GH * a + GH, :], ident)
                mm.then_inc(turn_full, 1)

            def scores_t(i, g):
                b, a = i // NG, i % NG
                n = GH * i + g
                pe.wait_ge(turn_free, full(f"qm{i}"))
                if n >= 2:
                    pe.wait_ge(exp_done, 2 * (n - 1))
                pair = 2 + 2 * (n % 2)
                for j in range(2):
                    pe.matmul(bank[pair + j][:, :], ident_b[:, :],
                              mbias_t[:, 2 * j:2 * j + 2, :].rearrange("p k q -> p (k q)"),
                              start=True, stop=False, skip_group_check=True)
                    for k in range(2):
                        at = b * SK + (2 * j + k) * P
                        mm = pe.matmul(bank[pair + j][:, k * S:(k + 1) * S], kx[:, a, g, at:at + P],
                                       qm_t[:, i % 2, :], start=False, stop=(k == 1), skip_group_check=True)
                mm.then_inc(st_ready, 1)

            def values(i):
                b, a = i // NG, i % NG
                pe.wait_ge(exp_done, 2 * GH * (i + 1))
                if i >= 1:
                    pe.wait_ge(pv_taken, i)
                for k in range(KT):
                    for g in range(GH):
                        mm = pe.matmul(bank[6][32 * g:32 * g + VROWS, 0:S], vx[:, b * KT + k, GH * a + g, :],
                                       pt[:, (GH * i + g) % (2 * GH), k * S:(k + 1) * S],
                                       start=(k == 0), stop=(k == KT - 1))
                mm.then_inc(pv_ready, 1)

            def turn_out(i):
                pe.wait_ge(pv_taken, i + 1)
                turn_begin(f"o{i}")
                for q in range(QT):
                    mm = pe.transpose(turn[:, q * P:(q + 1) * P], ot[:, i % 2, q * P:(q + 1) * P], ident)
                mm.then_inc(turn_full, 1)

            pe.wait_ge(qxt_taken, 4)
            pe.wait_ge(in_ones, 16 * H)
            pe.wait_ge(kx_rows, 16 * 3 * H)
            for g in range(GH):
                scores(0, g)
            pe.wait_ge(identb_ready, 1)
            pe.wait_ge(mt_taken, 2)
            pe.wait_ge(vx_pad, 2)
            pe.wait_ge(pv_zero, 1)
            for i in range(STEPS):
                turn_negmax(i)
                for g in range(GH):
                    if i + 1 < STEPS:
                        scores(i + 1, g)
                    scores_t(i, g)
                if i >= 2:
                    turn_out(i - 2)
                if i >= 1:
                    values(i - 1)
                if i == 6:
                    pe.wait_ge(att2_ready, NG)
                    turn_tiles("att2_t0", att2, 0)
                    pe.wait_ge(turn_free, full("att2_t0"))
                    turn_product("wo0", att2_t[:, :], cl("wo"), P)
                if i == 7:
                    pe.wait_ge(x2_ready, 1)
                    turn_tiles("x2_t0", x2, 0)
                    pe.wait_ge(turn_free, full("x2_t0"))
                    turn_product("gate0", x2_t[:, 0, :], cl("gate_w"), E)

            def up(u):
                b, e, hc = u // (EX * HC), u // HC % EX, u % HC
                if u >= 4:
                    pe.wait_ge(gelu_done, u - 3)
                pe.matmul(bank[u % 4][:, 0:S], w1s[:, e, hc * P:(hc + 1) * P], x2_t[:, b, :],
                          start=True, stop=True).then_inc(up_ready, 1)

            def down(u):
                b, e, hc = u // (EX * HC), u // HC % EX, u % HC
                o = u // HC
                pe.wait_ge(gelu_done, u + 1)
                if hc == 0 and o >= 2:
                    pe.wait_ge(acc_done, o - 1)
                for q in range(QT):
                    mm = pe.matmul(bank[4 + o % 2][:, q * P:(q + 1) * P], hs[:, u % 4, q * P:(q + 1) * P],
                                   w2s[:, e, hc, :], start=(hc == 0 and q == 0), stop=(hc == HC - 1),
                                   skip_group_check=True)
                mm.then_inc(down_done, 1)

            def turn_comb(b):
                pe.wait_ge(comb_ready, b + 1)
                turn_begin(f"comb_t{b}")
                for q in range(QT):
                    mm = pe.transpose(turn[0:EX, q * P:(q + 1) * P], comb[:, 2 * b + q, :], ident)
                mm.then_inc(turn_full, 1)

            def turn_b2(b):
                pe.wait_ge(turn_free, full(f"comb_t{b}"))
                turn_product(f"b2{b}", comb_t[0:EX, :], b2r[:, :], P)

            pe.wait_ge(in_w1, 16)
            pe.wait_ge(max_done, 2 * GH * STEPS)
            up(0)
            up(1)
            turn_out(6)
            values(7)
            turn_comb(0)
            pe.wait_ge(in_w2, 16)
            pe.wait_ge(in_b2, 16)
            for u in range(UNITS):
                if u + 2 < UNITS:
                    up(u + 2)
                down(u)
                if u == 3:
                    turn_out(7)
                if u == 5:
                    turn_b2(0)
                if u == 6:
                    pe.wait_ge(att2_ready, 2 * NG)
                    turn_tiles("att2_t1", att2, 1)
                if u == 9:
                    pe.wait_ge(turn_free, full("att2_t1"))
                    turn_product("wo1", att2_t[:, :], cl("wo"), P)
                if u == 14:
                    pe.wait_ge(x2_ready, 2)
                    turn_tiles("x2_t1", x2, 1)
                if u == 17:
                    pe.wait_ge(turn_free, full("x2_t1"))
                    turn_product("gate1", x2_t[:, 1, :], cl("gate_w"), E)
                if u == 24:
                    turn_comb(1)
                if u == 27:
                    turn_b2(1)

        @block.vector
        def _(dve):
            chain = [0]

            def link(ins):
                chain[0] += 1
                ins.then_inc(v_chain, 1)
                dve.wait_ge(v_chain, chain[0])

            def note(ins):
                chain[0] += 1
                ins.then_inc(v_chain, 1)
                return chain[0]

            dve.memset(kx[:, 0, :, :].bitcast(F32), 0.0).then_inc(kx_zero_v, 1)
            dve.memset(comb[:, :, E:EX], 1.0).then_inc(v_chain, 1)
            dve.memset(qx[:, :, :, 0:2], 0.0).then_inc(v_chain, 1)
            dve.memset(qx[:, :, :, 2 + 3 * D:QROWS], 0.0).then_inc(v_chain, 1)
            chain[0] += 3
            dve.wait_ge(in_row, 16)
            in_b, rel = rw("in_b"), rw("rel").rearrange("p (r d) -> p r d", r=3)
            for s in range(B):
                dve.tensor_copy(bias_qkkv[:, s, 0:P], in_b[:, 0:P]).then_inc(v_chain, 1)
                dve.tensor_copy(bias_qkkv[:, s, 3 * P:4 * P], in_b[:, 2 * P:3 * P]).then_inc(v_chain, 1)
                for t in range(B):
                    dve.tensor_tensor(bias_qkkv[:, s, (1 + t) * P:(2 + t) * P].rearrange("p (h d) -> p h d", h=H),
                                      in_b[:, P:2 * P].rearrange("p (h d) -> p h d", h=H),
                                      rel[:, s - t + 1, :].unsqueeze(1).broadcast_to([P, H, D]),
                                      ALU.add).then_inc(v_chain, 1)
                chain[0] += 4
            dve.wait_ge(v_chain, chain[0])
            for t in range(NT):
                dve.wait_ge(qkv_ready, t + 1)
                dve.tensor_tensor(qkkv[:, t, :], bank[t][:, :], bias_qkkv[:, t // QT, :], ALU.add)\
                    .then_inc(qkv_taken, 1)
            dve.wait_ge(qkv_taken, NT)
            for t in range(B):
                for s in range(B):
                    dve.tensor_tensor(prod[:, t, s, :].rearrange("p (q n) -> p q n", q=QT),
                                      qkkv[:, 2 * t:2 * t + 2, 0:P],
                                      qkkv[:, 2 * s:2 * s + 2, (1 + t) * P:(2 + t) * P], ALU.mult).then_inc(v_chain, 1)
            chain[0] += 4
            dve.wait_ge(v_chain, chain[0])
            link(dve.tensor_reduce(sc[:, :, :, :].rearrange("p t s n -> p (t s n)"),
                                   prod[:, :, :, :].rearrange("p t s (n d) -> p (t s n) d", d=D), AX.X, ALU.add))
            link(dve.tensor_tensor(smax[:, :, :], sc[:, :, 0, :], sc[:, :, 1, :], ALU.max))
            dve.tensor_tensor(sd[:, :, :, :], sc[:, :, :, :],
                              smax[:, :, :].unsqueeze(2).broadcast_to([P, B, B, QT * H]), ALU.subtract)\
                .then_inc(sd_ready, 1)
            dve.wait_ge(in_mask, 16)
            dve.wait_ge(in_col, 16)
            dve.tensor_copy(ident_b[:, :], ident).then_inc(identb_ready, 1)
            link(dve.tensor_scalar(nz[:, :, :], msk[:, :, :], 0.0, None, ALU.not_equal))
            link(dve.tensor_reduce(any_[:, :], nz[:, :, :], AX.X, ALU.max))
            dve.tensor_scalar(qsc[:, :], any_[:, :], HEAD_SCALE, None, ALU.mult).then_inc(v_chain, 1)
            chain[0] += 1
            link(dve.tensor_scalar(big[:, :], any_[:, :], -NEG, None, ALU.mult))
            for q in range(QT):
                dve.tensor_scalar(mbias[:, q, :], nz[:, q, :], -1.0, big[:, q:q + 1], ALU.add, ALU.mult)\
                    .then_inc(mbias_ready, 1)
                dve.tensor_scalar(bqs[:, q, :], rw("bq"), qsc[:, q:q + 1], None, ALU.mult).then_inc(v_chain, 1)
            chain[0] += 2
            dve.wait_ge(se_ready, 1)
            link(dve.tensor_tensor(ssum[:, :, :], se[:, :, 0, :], se[:, :, 1, :], ALU.add))
            link(dve.reciprocal(srec[:, :, :], ssum[:, :, :]))
            link(dve.tensor_tensor(sp_[:, :, :, :], se[:, :, :, :],
                                   srec[:, :, :].unsqueeze(2).broadcast_to([P, B, B, QT * H]), ALU.mult))
            for t in range(B):
                for s in range(B):
                    for q in range(QT):
                        dve.tensor_tensor(prod[:, t, s, q * P:(q + 1) * P].rearrange("p (h d) -> p h d", h=H),
                                          qkkv[:, 2 * s + q, 3 * P:4 * P].rearrange("p (h d) -> p h d", h=H),
                                          sp_[:, t, s, q * H:(q + 1) * H].unsqueeze(2).broadcast_to([P, H, D]),
                                          ALU.mult).then_inc(v_chain, 1)
                chain[0] += 4
                dve.wait_ge(v_chain, chain[0])
                dve.tensor_tensor(att[:, 2 * t:2 * t + 2, :].rearrange("p q n -> p (q n)"),
                                  prod[:, t, 0, :], prod[:, t, 1, :], ALU.add).then_inc(att_ready, 1)
            for b in range(B):
                dve.wait_ge(v_ready, b + 1)
                dve.tensor_tensor(vx[:, b * KT:(b + 1) * KT, :, 0:D],
                                  bank[6 + b][:, :].rearrange("p (k h d) -> p k h d", k=KT, h=H),
                                  rw("bv").rearrange("p (h d) -> p h d", h=H).unsqueeze(1)
                                  .broadcast_to([P, KT, H, D]), ALU.add).then_inc(v_taken, 1)
            dve.wait_ge(v_taken, 1)
            dve.memset(bank[6][:, 0:S], 0.0).then_inc(pv_zero, 1)
            dve.wait_ge(in_x, 16)
            link(dve.tensor_tensor(xb[:, :, :], xtok[:, :, :],
                                   rw("out_b").unsqueeze(1).broadcast_to([P, NT, P]), ALU.add))

            def norm(k, b, dst, done):
                for q in range(QT):
                    dve.bn_stats(stats[:, 2 * b + q, :], res[:, 2 * b + q, :]).then_inc(v_chain, 1)
                chain[0] += 2
                dve.wait_ge(v_chain, chain[0])
                for q in range(QT):
                    dve.bn_aggr(mv[:, 2 * b + q, :], stats[:, 2 * b + q, :]).then_inc(v_chain, 1)
                chain[0] += 2
                dve.wait_ge(v_chain, chain[0])
                dve.tensor_scalar(vare[:, 2 * b:2 * b + 2], mv[:, 2 * b:2 * b + 2, 1], LN_EPS, None, ALU.add)\
                    .then_inc(var_ready, 1)

            def norm_end(k, b, dst, done):
                dve.wait_ge(rstd_ready, k)
                for q in range(QT):
                    t = 2 * b + q
                    ins = dve.tensor_scalar(dst[:, t, :], res[:, t, :], mv[:, t, 0:1], rstd[:, t:t + 1],
                                            ALU.subtract, ALU.mult)
                    if q == 0:
                        ins.then_inc(v_chain, 1)
                        chain[0] += 1
                ins.then_inc(done, 1)

            for b in range(B):
                dve.wait_ge(turn_full, full(f"out_w{b}"))
                dve.tensor_tensor(res[:, 2 * b:2 * b + 2, :], turn[:, 0:S].rearrange("p (q n) -> p q n", q=QT),
                                  xb[:, 2 * b:2 * b + 2, :], ALU.add).then_inc(turn_free, 1)
                dve.wait_ge(turn_free, full(f"out_w{b}"))
                norm(b + 1, b, x1, x1_ready)
            for b in range(B):
                norm_end(b + 1, b, x1, x1_ready)
            for b in range(B):
                dve.wait_ge(turn_full, full(f"q{b}"))
                for q in range(QT):
                    ins = dve.scalar_tensor_tensor(qf[:, 2 * b + q, :], turn[:, q * P:(q + 1) * P], qsc[:, q:q + 1],
                                                   bqs[:, q, :], ALU.mult, ALU.add)
                    if q == 0:
                        ins.then_inc(v_chain, 1)
                        chain[0] += 1
                        dve.wait_ge(v_chain, chain[0])
                ins.then_inc(turn_free, 1)
                dve.wait_ge(turn_free, full(f"q{b}"))
                heads = qf[:, 2 * b:2 * b + 2, :].rearrange("p t (h d) -> p t h d", h=H)
                high = qx[:, 2 * b:2 * b + 2, :, 2:2 + D]
                dve.tensor_copy(high.bitcast(F32R), heads).then_inc(v_chain, 1)
                dve.tensor_copy(qx[:, 2 * b:2 * b + 2, :, 2 + D:2 + 2 * D].bitcast(F32R), heads).then_inc(v_chain, 1)
                chain[0] += 2
                dve.wait_ge(v_chain, chain[0])
                dve.tensor_tensor(qx[:, 2 * b:2 * b + 2, :, 2 + 2 * D:2 + 3 * D].bitcast(F32R), heads, high,
                                  ALU.subtract).then_inc(qx_ready, 1)
            link(dve.tensor_tensor(x1b[:, :, :], x1[:, :, :],
                                   rw("bo").unsqueeze(1).broadcast_to([P, NT, P]), ALU.add))

            def row_max(i):
                b, a = i // NG, i % NG
                for g in range(GH):
                    for q in range(QT):
                        n = 2 * (GH * i + g) + q
                        dve.wait_ge(s_ready, n + 1)
                        if n >= 4:
                            dve.wait_ge(max_done, n - 3)
                        h = GH * a + g
                        dve.tensor_tensor_reduce(junk[:, n % 4, :], bank[n % 2][:, :], mbias[:, q, :], 1.0, LOWEST,
                                                 ALU.add, ALU.max, rowmax[:, 2 * b + q, h:h + 1]).then_inc(max_done, 1)
                dve.wait_ge(max_done, 2 * GH * (i + 1))
                dve.wait_ge(qxt_ready, 4)
                m = rowmax[:, 2 * b:2 * b + 2, GH * a:GH * a + GH]
                high = qx[:, 2 * b:2 * b + 2, GH * a:GH * a + GH, 0:1]
                low = qx[:, 2 * b:2 * b + 2, GH * a:GH * a + GH, 1:2]
                link(dve.tensor_scalar(high.bitcast(F32R), m.unsqueeze(3), -1.0, None, ALU.mult))
                for q in range(QT):
                    ins = dve.scalar_tensor_tensor(low[:, q].bitcast(F32R), m[:, q].unsqueeze(2), -1.0, high[:, q],
                                                   ALU.mult, ALU.subtract)
                    if q == 0:
                        ins.then_inc(v_chain, 1)
                        chain[0] += 1
                ins.then_inc(negmax_ready, 1)

            def take_out(i):
                b, a = i // NG, i % NG
                dve.wait_ge(turn_full, full(f"o{i}"))
                o = turn[:, 0:S].rearrange("p (q g r) -> p q g r", q=QT, g=GH)
                link(dve.reciprocal(orec[:, :, :].unsqueeze(3), o[:, :, :, D:D + 1]))
                dst = att2[:, 2 * b:2 * b + 2, a * GH * D:(a + 1) * GH * D].rearrange("p q (g d) -> p q g d", g=GH)
                dve.tensor_tensor(dst, o[:, :, :, 0:D], orec[:, :, :].unsqueeze(3).broadcast_to([P, QT, GH, D]),
                                  ALU.mult).then_inc(att2_ready, 1)
                dve.wait_ge(att2_ready, i + 1)
                dve.sem_inc(turn_free, 1)

            def after_attention(b):
                dve.wait_ge(turn_full, full(f"wo{b}"))
                dve.tensor_tensor(res[:, 2 * b:2 * b + 2, :], turn[:, 0:S].rearrange("p (q n) -> p q n", q=QT),
                                  x1b[:, 2 * b:2 * b + 2, :], ALU.add).then_inc(turn_free, 1)
                dve.wait_ge(turn_free, full(f"wo{b}"))
                norm(3 + b, b, x2, x2_ready)

            def router(b):
                two = slice(2 * b, 2 * b + 2)
                dve.wait_ge(turn_full, full(f"gate{b}"))
                dve.tensor_tensor(logit[:, two, :], turn[:, 0:S].rearrange("p (q n) -> p q n", q=QT)[:, :, 0:E],
                                  rw("gate_b").unsqueeze(1).broadcast_to([P, QT, E]), ALU.add).then_inc(turn_free, 1)
                dve.wait_ge(turn_free, full(f"gate{b}"))
                for t in range(2 * b, 2 * b + 2):
                    link(dve.max(top[:, t, :], logit[:, t, :]))
                    link(dve.max_index(topi[:, t, :], top[:, t, :], logit[:, t, :]))
                dve.tensor_copy(topf[:, two, :], topi[:, two, 0:2]).then_inc(v_chain, 1)
                chain[0] += 1
                dve.tensor_tensor(gap[:, two], top[:, two, 1], top[:, two, 0], ALU.subtract).then_inc(gap_ready, 1)

            def router_end(b):
                two = slice(2 * b, 2 * b + 2)
                dve.wait_ge(e2_ready, b + 1)
                link(dve.tensor_scalar(den[:, two], e2[:, two], 1.0, None, ALU.add))
                link(dve.reciprocal(gw[:, two, 0], den[:, two]))
                link(dve.tensor_tensor(gw[:, two, 1], e2[:, two], gw[:, two, 0], ALU.mult))
                for t in range(2 * b, 2 * b + 2):
                    link(dve.tensor_scalar(hot[:, t, :], rw("iota"), topf[:, t, 0:1], gw[:, t, 0:1],
                                           ALU.is_equal, ALU.mult))
                    link(dve.tensor_scalar(comb[:, t, 0:E], rw("iota"), topf[:, t, 1:2], gw[:, t, 1:2],
                                           ALU.is_equal, ALU.mult))
                    ins = dve.tensor_tensor(comb[:, t, 0:E], comb[:, t, 0:E], hot[:, t, :], ALU.add)
                    if t == 2 * b:
                        link(ins)
                ins.then_inc(comb_ready, 1)
                dve.wait_ge(comb_ready, b + 1)

            def acc_init(b):
                dve.wait_ge(turn_full, full(f"b2{b}"))
                dve.tensor_tensor(acc[:, 2 * b:2 * b + 2, :], turn[:, 0:S].rearrange("p (q n) -> p q n", q=QT),
                                  x2[:, 2 * b:2 * b + 2, :], ALU.add).then_inc(turn_free, 1)
                dve.wait_ge(turn_free, full(f"b2{b}"))

            def accumulate(o):
                b, e = o // EX, o % EX
                if o:
                    dve.wait_ge(acc_done, o)
                dve.wait_ge(down_done, HC * (o + 1))
                dst = res if e == EX - 1 else acc
                for q in range(QT):
                    t = 2 * b + q
                    ins = dve.scalar_tensor_tensor(dst[:, t, :], bank[4 + o % 2][:, q * P:(q + 1) * P],
                                                   comb[:, t, e:e + 1], acc[:, t, :], ALU.mult, ALU.add)
                    if q == 0:
                        link(ins)
                ins.then_inc(acc_done, 1)

            dve.wait_ge(mbias_ready, QT)
            row_max(0)
            for i in range(STEPS):
                if i + 1 < STEPS:
                    row_max(i + 1)
                if i >= 2:
                    take_out(i - 2)
                if i == 6:
                    after_attention(0)
                    norm_end(3, 0, x2, x2_ready)
                if i == 7:
                    router(0)
                    router_end(0)
            take_out(6)
            take_out(7)
            acc_init(0)
            accumulate(0)
            after_attention(1)
            accumulate(1)
            norm_end(4, 1, x2, x2_ready)
            accumulate(2)
            accumulate(3)
            router(1)
            router_end(1)
            accumulate(4)
            accumulate(5)
            acc_init(1)
            for o in range(6, B * EX):
                accumulate(o)
                if o == EX - 1 or o == 2 * EX - 1:
                    b = o // EX
                    dve.wait_ge(acc_done, o + 1)
                    norm(5 + b, b, fin, fin_ready)
                    norm_end(5 + b, b, fin, fin_ready)


_OUT = ((B, S, P), "float32")


def kernel(**inputs):
    import numpy as np
    import concourse.bacc as bacc
    from concourse.bass_utils import run_bass_kernel_spmd

    def a(name):
        return np.asarray(inputs[name])

    x, c = a("x"), a("ctx_1024")
    w = a("L0_attn_in_proj_weight").T
    arrays = {
        "x_t_w": np.concatenate([x.reshape(B * S, P).T, w[:, 0:2 * P], w[:, P:3 * P]], axis=1),
        "x_tok": x.reshape(NT, P, P).transpose(1, 0, 2),
        "ctx_w": np.concatenate([c.reshape(B * SK, P).T, a("L0_xattn_wk").T, a("L0_xattn_wv").T], axis=1),
        "cols": np.concatenate([
            np.eye(P, dtype=np.float32), a("L0_attn_out_w").T, a("L0_xattn_wq").T, a("L0_xattn_wo").T,
            a("L0_ffn_gate_w"), a("L0_ffn_b1").reshape(E * HC, P).T, a("L0_ffn_bs1").reshape(HC, P).T,
            a("L0_xattn_bk").reshape(P, 1)], axis=1),
        "rows": np.concatenate([
            a("L0_attn_in_proj_bias"), a("L0_attn_rel_pos_keys")[REL - 1:REL + 2, 0:D].reshape(-1),
            a("L0_attn_out_b"), a("L0_xattn_bq"), a("L0_xattn_bv"), a("L0_xattn_bo"), a("L0_ffn_gate_b"),
            np.arange(E, dtype=np.float32), np.full(4, np.e, np.float32), np.full(4, -0.5, np.float32)])[None, :],
        "b2_rows": np.concatenate([a("L0_ffn_b2"), a("L0_ffn_bs2")[None, :]], axis=0),
        "mask": a("mask_1x1xSxS2_ik0").reshape(QT, P, SK).transpose(1, 0, 2),
        "w1": np.concatenate([a("L0_ffn_w1"), a("L0_ffn_ws1")[None]], axis=0).transpose(1, 0, 2),
        "w2": np.concatenate([a("L0_ffn_w2"), a("L0_ffn_ws2")[None]], axis=0)
              .reshape(EX, HC, P, P).transpose(2, 0, 1, 3),
    }
    arrays = {k: np.ascontiguousarray(v) for k, v in arrays.items()}
    nc = bacc.Bacc("TRN2", target_bir_lowering=False, num_devices=1)
    aps = {k: nc.dram_tensor(k, v.shape, mybir.dt.from_np(v.dtype), kind="ExternalInput").ap()
           for k, v in arrays.items()}
    aps["rows"] = aps["rows"].broadcast_to([P, ROW_N])
    y = nc.dram_tensor("y", _OUT[0], F32, kind="ExternalOutput").ap()
    decoder_layer(nc, *aps.values(), y)
    r = run_bass_kernel_spmd(nc, [arrays], core_ids=[0])
    return r.results[0]["y"]
```

```python
from contextlib import ExitStack

import concourse.bass as bass
from concourse import mybir

F32 = mybir.dt.float32
F32R = mybir.dt.float32r
BF16 = mybir.dt.bfloat16
I32 = mybir.dt.int32
U32 = mybir.dt.uint32
ALU = mybir.AluOpType
ACT = mybir.ActivationFunctionType
AX = mybir.AxisListType

P = 128
B = 2
S = 256
SK = 512
H = 16
D = P // H
NT = B * S // P
QT = S // P
KT = SK // P
E = 8
EX = E + 1
HID = 512
HC = HID // P
GH = 4
NG = H // GH
QROWS = 32
KROWS = 2 + 3 * D
VROWS = 16
STEPS = B * NG
LN_EPS = 1e-5
HEAD_SCALE = float(D) ** -0.5
NEG = -1e9
LOWEST = -3.0e38
WARM = 32
KEEP = (8, 2, 3, 4, 2, 6, 3, 2, 6)
REL = 16

PROJ_W = 4 * P
ROW = {}
_at = 0
for _name, _n in (("in_b", 3 * P), ("rel", 3 * D), ("out_b", P), ("bq", P), ("bv", P), ("bo", P),
                  ("gate_b", E), ("iota", E), ("e", 4), ("minus_half", 4)):
    ROW[_name] = (_at, _at + _n)
    _at += _n
ROW_N = _at
COL = {}
_at = 0
for _name, _n in (("ident", P), ("out_w", P), ("wq", P), ("wo", P), ("gate_w", E), ("b1", EX * HC), ("bk", 1)):
    COL[_name] = (_at, _at + _n)
    _at += _n
COL_N = _at


def decoder_layer(nc, x_t_w, x_tok, ctx_w, cols, rows, b2_rows, mask, w1, w2, heads, out):
    with ExitStack() as ctx:
        def sb(name, shape, dt=F32):
            return ctx.enter_context(nc.sbuf_tensor(name, shape, dt))

        def sem(name):
            return ctx.enter_context(nc.semaphore(name))

        def views(region, *shapes):
            out, at = [], 0
            for shape in shapes:
                n = 1
                for k in shape:
                    n *= k
                v = region[:, at:at + n]
                names = "abcd"[:len(shape)]
                if len(shape) > 1:
                    v = v.rearrange(f"p ({' '.join(names)}) -> p {' '.join(names)}", **dict(zip(names, shape)))
                out.append(v)
                at += n
            assert at <= region.shape[1]
            return out

        region_p = sb("region_p", [P, 2 * GH * KT * S])
        region_m = sb("region_m", [P, QT * SK + B * PROJ_W])
        region_n = sb("region_n", [P, QT * SK])
        region_x = sb("region_x", [P, B * S + PROJ_W])
        region_j = sb("region_j", [P, 4 * SK // 2])
        region_b = sb("region_b", [P, NT * P])
        region_t = sb("region_t", [P, NT * P])
        [xw] = views(region_x, (B * S + PROJ_W,))
        kf, kh_, kl_, cw, qkkv, prod, xtok = views(
            region_p, (B * SK,), (B * SK,), (B * SK,), (B * SK + 2 * P,),
            (NT, PROJ_W), (B, B, QT * P),
            (NT, P))
        kh, kl = kh_.bitcast(F32R), kl_.bitcast(F32R)
        col = sb("col", [P, COL_N])
        row = sb("row", [P, ROW_N])
        b2r = sb("b2r", [EX, P])
        msk, bias_qkkv = views(region_m, (QT, SK), (B, PROJ_W))
        msk = msk.bitcast(I32)
        w1s = sb("w1s", [P, EX, HID])
        w2s = sb("w2s", [P, EX, HC, P])

        def rw(name):
            return row[:, ROW[name][0]:ROW[name][1]]

        def cl(name):
            return col[:, COL[name][0]:COL[name][1]]

        ident = cl("ident")
        sc = sb("sc", [P, B, B, QT * H])
        smax = sb("smax", [P, B, QT * H])
        sd = sb("sd", [P, B, B, QT * H])
        se = sb("se", [P, B, B, QT * H])
        ssum = sb("ssum", [P, B, QT * H])
        srec = sb("srec", [P, B, QT * H])
        sp_ = sb("sp_", [P, B, B, QT * H])
        [ones] = views(region_j, (B * SK,))
        att, att_t = views(region_x, (NT, P), (NT * P,))
        [xb] = views(region_b, (NT, P))
        res = sb("res", [P, NT, P])
        stats = sb("stats", [P, NT, 6])
        mv = sb("mv", [P, NT, 2])
        vare = sb("vare", [P, NT])
        rstd = sb("rstd", [P, NT])
        x1 = sb("x1", [P, NT, P])
        [x1b] = views(region_b, (NT, P))
        [x1_t] = views(region_t, (NT * P,))
        [gone] = views(region_n, (QT, SK))
        none_ = sb("none_", [P, QT])
        any_ = sb("any_", [P, QT])
        qsc = sb("qsc", [P, QT])
        big = sb("big", [P, QT])
        bqs = sb("bqs", [P, QT, P])
        mbias = sb("mbias", [P, QT, SK])
        mbias_t = sb("mbias_t", [P, KT, S], BF16)
        ident_b = sb("ident_b", [P, P], BF16)
        kx = sb("kx", [P, NG, GH, B * SK], F32R)
        vx = sb("vx", [P, B * KT, H, VROWS])
        qf = sb("qf", [P, NT, P])
        qx = sb("qx", [P, NT, H, QROWS])
        qx_t = sb("qx_t", [P, NG, NT * P], F32R)
        qm_t = sb("qm_t", [P, 2, S], F32R)
        junk = region_j[:, :].bitcast(BF16).rearrange("p (n k) -> p n k", n=4)
        rowmax = sb("rowmax", [P, NT, H])
        [pt] = views(region_p, (2 * GH, KT * S))
        orec = sb("orec", [P, QT, GH])
        att2, ot = views(region_x, (NT, P), (2, S))
        [att2_t, comb_t] = views(region_t, (S,), (S,))
        x2, x2_t = views(region_n, (NT, P), (B, S))
        logit = sb("logit", [P, NT, E])
        top = sb("top", [P, NT, 8])
        topi = sb("topi", [P, NT, 8], U32)
        topf = sb("topf", [P, NT, 2])
        gap = sb("gap", [P, NT])
        e2 = sb("e2", [P, NT])
        den = sb("den", [P, NT])
        gw = sb("gw", [P, NT, 2])
        hot = sb("hot", [P, NT, E])
        comb = sb("comb", [P, NT, EX])
        hs, acc, fin = views(region_m, (4, S), (NT, P), (NT, P))

        kx_flat = kx[:, :, :, :].rearrange("p a g n -> p (a g n)")
        w1h = [kx_flat[:, 2 * HID * e:2 * HID * e + HID] for e in range(EX)]
        w1l = [kx_flat[:, 2 * HID * e + HID:2 * HID * (e + 1)] for e in range(EX)]
        x2h, x2l = [kx_flat[:, 2 * HID * EX + B * S * k:2 * HID * EX + B * S * (k + 1)]
                    .rearrange("p (b n) -> p b n", b=B) for k in range(2)]
        bank = [ctx.enter_context(nc.psum_tensor(f"bank{i}", [P, 512], F32)) for i in range(8)]
        turn = bank[7]

        in_row, in_xw, in_cw, in_col = sem("in_row"), sem("in_xw"), sem("in_cw"), sem("in_col")
        in_x, in_mask, in_w1, in_w2, in_b2 = sem("in_x"), sem("in_mask"), sem("in_w1"), sem("in_w2"), sem("in_b2")
        ones_ready, in_ones, heads_done, kx_rows, out_done = sem("ones_ready"), sem("in_ones"), sem("heads_done"), sem("kx_rows"), sem("out_done")
        qkv_ready, qkv_taken = sem("qkv_ready"), sem("qkv_taken")
        sd_ready, se_ready = sem("sd_ready"), sem("se_ready")
        gone_ready, qx_pad = sem("gone_ready"), sem("qx_pad")
        w1h_ready, w1l_ready, x2t_ready, x2l_ready = (
            sem("w1h_ready"), sem("w1l_ready"), sem("x2t_ready"), sem("x2l_ready"))
        att_ready = sem("att_ready")
        var_ready, rstd_ready = sem("var_ready"), sem("rstd_ready")
        x1_ready, xb_ready, x1b_ready = sem("x1_ready"), sem("xb_ready"), sem("x1b_ready")
        kt_ready, kt_taken = sem("kt_ready"), sem("kt_taken")
        v_ready, v_taken = sem("v_ready"), sem("v_taken")
        kx_zero_v, kx_zero_g, kx_zero_a, vx_pad = sem("kx_zero_v"), sem("kx_zero_g"), sem("kx_zero_a"), sem("vx_pad")
        kl_ready, identb_ready = sem("kl_ready"), sem("identb_ready")
        mbias_ready, mt_ready, mt_taken = sem("mbias_ready"), sem("mt_ready"), sem("mt_taken")
        qx_ready, qxt_ready, qxt_taken = sem("qx_ready"), sem("qxt_ready"), sem("qxt_taken")
        turn_full, turn_free = sem("turn_full"), sem("turn_free")
        s_ready, max_done, negmax_ready = sem("s_ready"), sem("max_done"), sem("negmax_ready")
        st_ready, exp_done = sem("st_ready"), sem("exp_done")
        pv_ready, pv_taken, pv_zero = sem("pv_ready"), sem("pv_taken"), sem("pv_zero")
        x2_ready, comb_ready = sem("x2_ready"), sem("comb_ready")
        gap_ready, e2_ready = sem("gap_ready"), sem("e2_ready")
        up_ready, gelu_done, down_done, acc_done = sem("up_ready"), sem("gelu_done"), sem("down_done"), sem("acc_done")
        fin_ready = sem("fin_ready")
        warm_ready = sem("warm_ready")
        v_chain, g_chain = sem("v_chain"), sem("g_chain")

        inside = {(0, 2): "att_t1", (1, 0): "out_w1", (1, 3): "x1_t1", (2, 0): "q1", (2, 2): "qt2", (2, 3): "qt3",
                  (3, 0): "o0", (6, 0): "att2_t0", (6, 1): "wo0", (7, 0): "x2_t0", (7, 1): "gate0", (7, 3): "o6"}
        for i in range(3, STEPS):
            inside[i, 2] = f"o{i - 2}"
        turns = ["att_t0", "out_w0", "x1_t0", "q0", "qm0"]
        for i in range(STEPS):
            turns += [inside[i, g] for g in range(GH) if (i, g) in inside]
            if i + 1 < STEPS:
                turns.append(f"qm{i + 1}")
        turns += ["o7", "comb_t0", "b20", "att2_t1", "wo1", "x2_t1", "gate1", "comb_t1", "b21"]
        turn_no = {what: k for k, what in enumerate(turns)}

        def full(what):
            return turn_no[what] + 1

        UNITS = B * EX * HC
        AHEAD = 3
        block = ctx.enter_context(nc.Block())

        def score_bank(n):
            return bank[(0, 1, 4, 5)[n % 4]] if n < 2 * GH else bank[n % 2]

        @block.sync
        def _(sp):
            sp.dma_start(xw[:, :], x_t_w).then_inc(in_xw, 16)
            sp.dma_start(cw[:, :], ctx_w).then_inc(in_cw, 16)
            sp.dma_start(col[:, :], cols).then_inc(in_col, 16)
            sp.dma_start(xtok[:, :, :], x_tok).then_inc(in_x, 16)
            sp.dma_start(msk[:, :, :], mask).then_inc(in_mask, 16)
            sp.wait_ge(ones_ready, 1)
            sp.wait_ge(kx_zero_v, 1)
            sp.wait_ge(kx_zero_a, 1)
            sp.wait_ge(kx_zero_g, 1)
            for g in range(GH):
                sp.dma_start(kx[32 * g:32 * g + 2, :, g, :].bitcast(F32),
                             ones[0:2, :].unsqueeze(1).broadcast_to([2, NG, B * SK])).then_inc(in_ones, 16)
            parts = heads.rearrange("h d j n -> (h d) j n")
            sp.wait_ge(kt_taken, 4)
            for j in (0, 2):
                sp.dma_start(parts[:, j, :], kh_[:, :]).then_inc(heads_done, 16)
            sp.wait_ge(kl_ready, 1)
            sp.dma_start(parts[:, 1, :], kl_[:, :]).then_inc(heads_done, 16)
            sp.wait_ge(heads_done, 16 * 3)
            for g in range(GH):
                sp.dma_start(kx[32 * g + 2:32 * g + KROWS, :, g, :].bitcast(F32),
                             heads.rearrange("(a g) d j n -> g (d j) a n", g=GH)[g]).then_inc(kx_rows, 16)
            sp.dma_start(w1s[:, :, :], w1).then_inc(in_w1, 16)
            sp.dma_start(b2r[:, :], b2_rows).then_inc(in_b2, 16)
            sp.dma_start(w2s[:, :, :, :], w2).then_inc(in_w2, 16)
            for b in range(B):
                sp.wait_ge(fin_ready, b + 1)
                sp.dma_start(out[b].rearrange("(t p) d -> p t d", p=P), fin[:, 2 * b:2 * b + 2, :])\
                    .then_inc(out_done, 16)
            sp.wait_ge(out_done, 16 * B)

        @block.gpsimd
        def _(pool):
            pool.memset(ones[0:2, :], 1.0).then_inc(ones_ready, 1)
            pool.memset(kx[:, 2:4, :, :].bitcast(F32), 0.0).then_inc(kx_zero_g, 1)
            pool.wait_ge(in_row, 16)
            pool.wait_ge(in_x, 16)
            pool.tensor_tensor(xb[:, :, :], xtok[:, :, :], rw("out_b").unsqueeze(1).broadcast_to([P, NT, P]),
                               ALU.add).then_inc(xb_ready, 1)
            pool.wait_ge(in_mask, 16)
            pool.tensor_scalar(gone[:, :, :], msk[:, :, :], 0.0, None, ALU.is_equal).then_inc(gone_ready, 1)
            pool.wait_ge(kt_taken, 4)
            pool.tensor_tensor(kl[:, :], kf[:, :], kh[:, :].bitcast(F32), ALU.subtract).then_inc(kl_ready, 1)
            pool.memset(qx[:, :, :, 0:2], 0.0).then_inc(qx_pad, 1)
            pool.memset(qx[:, :, :, 2 + 3 * D:QROWS], 0.0).then_inc(qx_pad, 1)
            pool.memset(vx[:, :, :, D:D + 1], 1.0).then_inc(vx_pad, 1)
            pool.memset(vx[:, :, :, D + 1:VROWS], 0.0).then_inc(vx_pad, 1)
            pool.memset(comb[:, :, E:EX], 1.0).then_inc(vx_pad, 1)

            def inv_sqrt(k, t0):
                pool.wait_ge(var_ready, k)
                pool.tensor_tensor(rstd[:, t0:t0 + 2], vare[:, t0:t0 + 2], rw("minus_half")[:, 0:2], ALU.pow)\
                    .then_inc(rstd_ready, 1)

            def router_exp(b):
                pool.wait_ge(gap_ready, b + 1)
                pool.tensor_tensor(e2[:, 2 * b:2 * b + 2], rw("e")[:, 0:2], gap[:, 2 * b:2 * b + 2], ALU.pow)\
                    .then_inc(e2_ready, 1)

            def w1_low(e):
                pool.wait_ge(w1h_ready, e + 1)
                pool.tensor_tensor(w1l[e], w1s[:, e, :], w1h[e].bitcast(F32), ALU.subtract).then_inc(w1l_ready, 1)

            inv_sqrt(1, 0)
            inv_sqrt(2, 2)
            pool.wait_ge(x1_ready, 2)
            pool.tensor_tensor(x1b[:, :, :], x1[:, :, :], rw("bo").unsqueeze(1).broadcast_to([P, NT, P]),
                               ALU.add).then_inc(x1b_ready, 1)
            for e in range(0, 4):
                w1_low(e)
            inv_sqrt(3, 0)
            for e in range(4, 8):
                w1_low(e)
            router_exp(0)
            w1_low(8)
            inv_sqrt(4, 2)
            router_exp(1)
            inv_sqrt(5, 0)
            inv_sqrt(6, 2)

        @block.scalar
        def _(act):
            act.dma_start(row[:, :], rows).then_inc(in_row, 16)

            act.wait_ge(kx_zero_v, 1)
            act.activation(kx[:, 1, :, :], kx[:, 0, :, :].bitcast(F32), ACT.Copy).then_inc(kx_zero_a, 1)
            act.wait_ge(in_col, 16)
            for b in range(B):
                act.wait_ge(kt_ready, b + 1)
                act.activation(kf[:, b * SK:(b + 1) * SK], bank[4 + b][:, :], ACT.Identity, bias=cl("bk"))\
                    .then_inc(kt_taken, 1)
                act.activation(kh[:, b * SK:(b + 1) * SK], bank[4 + b][:, :], ACT.Identity, bias=cl("bk"))\
                    .then_inc(kt_taken, 1)
            def self_exp(t):
                act.wait_ge(sd_ready, t + 1)
                act.activation(se[:, t, :, :], sd[:, t, :, :], ACT.Exp, scale=HEAD_SCALE).then_inc(se_ready, 1)

            def take(what, dst, src):
                act.wait_ge(turn_full, full(what))
                act.activation(dst, src, ACT.Copy).then_inc(turn_free, 1)

            def take_x2(b):
                act.wait_ge(turn_full, full(f"x2_t{b}"))
                act.activation(x2_t[:, b, :], turn[:, 0:S], ACT.Copy).then_inc(x2t_ready, 1)
                act.activation(x2h[:, b, :], turn[:, 0:S], ACT.Copy).then_inc(turn_free, 1)

            def take_values(i):
                if i >= 2:
                    act.wait_ge(turn_full, full(f"o{i - 2}"))
                act.wait_ge(pv_ready, i + 1)
                act.activation(ot[:, i % 2, :], bank[6][:, 0:S], ACT.Copy).then_inc(pv_taken, 1)

            self_exp(0)
            take("att_t0", att_t[:, 0:S], turn[:, 0:S])
            for half in range(2):
                act.wait_ge(mt_ready, half + 1)
                act.activation(mbias_t[:, 2 * half:2 * half + 2, :].rearrange("p k q -> p (k q)"),
                               bank[1 + 2 * half][:, :], ACT.Copy).then_inc(mt_taken, 1)
            take("x1_t0", x1_t[:, 0:S], turn[:, 0:S])
            self_exp(1)
            for pair in range(2):
                act.wait_ge(qxt_ready, pair + 1)
                act.activation(qx_t[:, 2 * pair:2 * pair + 2, 0:S],
                               bank[2 + pair][:, :].rearrange("p (a q) -> p a q", a=2), ACT.Copy)\
                    .then_inc(qxt_taken, 1)
            for i in range(STEPS):
                for g in range(GH):
                    n = GH * i + g
                    act.wait_ge(st_ready, n + 1)
                    if i >= 2:
                        act.wait_ge(pv_ready, i - 1)
                    pair = 2 + 2 * (n % 2)
                    for j in range(2):
                        act.activation(pt[:, n % (2 * GH), 512 * j:512 * j + 512], bank[pair + j][:, :], ACT.Exp)\
                            .then_inc(exp_done, 1)
                    if g == 0 and i >= 2:
                        take_values(i - 2)
                    what = inside.get((i, g))
                    if what == "att_t1":
                        take(what, att_t[:, S:2 * S], turn[:, 0:S])
                    if what == "x1_t1":
                        take(what, x1_t[:, S:2 * S], turn[:, 0:S])
                    if what in ("qt2", "qt3"):
                        pair = int(what[2]) - 2
                        take(what, qx_t[:, 2 * pair:2 * pair + 2, S:2 * S],
                             turn[:, :].rearrange("p (a q) -> p a q", a=2))
                    if what == "att2_t0":
                        take(what, att2_t[:, :], turn[:, 0:S])
                    if what == "x2_t0":
                        take_x2(0)
                    e = GH * (i - 5) + g
                    if e == 0:
                        act.wait_ge(in_w1, 16)
                    if 0 <= e < EX:
                        act.wait_ge(st_ready, GH * (5 + e // GH))
                        act.activation(w1h[e], w1s[:, e, :], ACT.Copy).then_inc(w1h_ready, 1)
                    if (i, g) == (STEPS - 1, 2):
                        take_values(STEPS - 2)
            for u in range(UNITS):
                b, e, hc = u // (EX * HC), u // HC % EX, u % HC
                act.wait_ge(up_ready, u + 1)
                if u >= 4:
                    act.wait_ge(down_done, u - 3)
                act.activation(hs[:, u % 4, :], bank[u % 4][:, 0:S], ACT.Gelu,
                               bias=col[:, COL["b1"][0] + e * HC + hc:COL["b1"][0] + e * HC + hc + 1])\
                    .then_inc(gelu_done, 1)
                if u == 1:
                    take_values(STEPS - 1)
                if u == 4:
                    take("comb_t0", comb_t[0:EX, :], turn[0:EX, 0:S])
                if u == 8:
                    take("att2_t1", att2_t[:, :], turn[:, 0:S])
                if u == 16:
                    take_x2(1)
                if u == 26:
                    take("comb_t1", comb_t[0:EX, :], turn[0:EX, 0:S])

        @block.tensor
        def _(pe):
            def turn_begin(what):
                if turn_no[what]:
                    pe.wait_ge(turn_free, turn_no[what])

            pe.wait_ge(warm_ready, 1)
            for k in range(WARM):
                pe.matmul(turn[:, 0:P], ident_b[:, :], ident_b[:, :], start=True, stop=True)

            def keep_clock(n, into):
                for k in range(n):
                    pe.matmul(into[:, 0:P], ident, ident, start=True, stop=True)

            pe.wait_ge(in_xw, 16)
            for t in range(NT):
                pe.matmul(bank[t][:, :], xw[:, t * P:(t + 1) * P], xw[:, B * S:B * S + PROJ_W],
                          start=True, stop=True).then_inc(qkv_ready, 1)
            pe.wait_ge(in_cw, 16)
            for b in range(B):
                pe.matmul(bank[4 + b][:, :], cw[:, B * SK:B * SK + P], cw[:, b * SK:(b + 1) * SK],
                          start=True, stop=True).then_inc(kt_ready, 1)
            for b in range(B):
                if b == 1:
                    pe.wait_ge(qkv_taken, 1)
                for k in range(KT):
                    mm = pe.matmul(bank[6 * (1 - b)][:, k * P:(k + 1) * P],
                                   cw[:, (b * KT + k) * P:(b * KT + k + 1) * P],
                                   cw[:, B * SK + P:B * SK + 2 * P], start=True, stop=True)
                mm.then_inc(v_ready, 1)

            def masks_t():
                pe.wait_ge(mbias_ready, QT)
                pe.wait_ge(qkv_taken, NT)
                for half in range(2):
                    for k in range(2):
                        for q in range(QT):
                            kt = 2 * half + k
                            mm = pe.transpose(bank[1 + 2 * half][:, (k * QT + q) * P:(k * QT + q + 1) * P],
                                              mbias[:, q, kt * P:(kt + 1) * P], ident)
                    mm.then_inc(mt_ready, 1)

            def turn_tiles(what, src, b):
                turn_begin(what)
                for q in range(QT):
                    mm = pe.transpose(turn[:, q * P:(q + 1) * P], src[:, 2 * b + q, :], ident)
                mm.then_inc(turn_full, 1)

            def turn_product(what, lhs, rhs, n):
                turn_begin(what)
                for q in range(QT):
                    mm = pe.matmul(turn[:, q * P:q * P + n], lhs[:, q * P:(q + 1) * P], rhs, start=True, stop=True)
                mm.then_inc(turn_full, 1)

            def parts_t(dst, b, pair, done):
                for a2 in range(2):
                    for q in range(QT):
                        a = 2 * pair + a2
                        mm = pe.transpose(dst[:, (a2 * QT + q) * P:(a2 * QT + q + 1) * P],
                                          qx[:, 2 * b + q, GH * a:GH * a + GH, :], ident)
                mm.then_inc(done, 1)

            def issue(what):
                b = int(what[-1])
                if what.startswith("att_t"):
                    pe.wait_ge(att_ready, b + 1)
                    turn_tiles(what, att, b)
                elif what.startswith("out_w"):
                    pe.wait_ge(turn_free, full(f"att_t{b}"))
                    turn_product(what, att_t[:, b * S:(b + 1) * S], cl("out_w"), P)
                elif what.startswith("x1_t"):
                    pe.wait_ge(x1_ready, b + 1)
                    turn_tiles(what, x1, b)
                elif what.startswith("qt"):
                    pe.wait_ge(qx_ready, 2)
                    turn_begin(what)
                    parts_t(turn, 1, b - 2, turn_full)
                elif what.startswith("q"):
                    pe.wait_ge(turn_free, full(f"x1_t{b}"))
                    turn_product(what, x1_t[:, b * S:(b + 1) * S], cl("wq"), P)
                elif what.startswith("o"):
                    turn_out(b)
                elif what.startswith("att2_t"):
                    pe.wait_ge(turn_free, full(f"o{NG * (b + 1) - 1}"))
                    turn_tiles(what, att2, b)
                elif what.startswith("wo"):
                    pe.wait_ge(turn_free, full(f"att2_t{b}"))
                    turn_product(what, att2_t[:, :], cl("wo"), P)
                elif what.startswith("x2_t"):
                    pe.wait_ge(x2_ready, b + 1)
                    turn_tiles(what, x2, b)
                elif what.startswith("gate"):
                    pe.wait_ge(turn_free, full(f"x2_t{b}"))
                    turn_product(what, x2_t[:, b, :], cl("gate_w"), E)

            pe.wait_ge(in_col, 16)
            keep_clock(KEEP[0], turn)
            issue("att_t0")
            pe.wait_ge(kt_taken, 4)
            keep_clock(KEEP[1], bank[5])
            issue("out_w0")
            keep_clock(KEEP[2], bank[5])
            masks_t()
            keep_clock(KEEP[3], bank[5])
            issue("x1_t0")
            keep_clock(KEEP[4], bank[5])
            issue("q0")
            keep_clock(KEEP[5], bank[5])
            pe.wait_ge(mt_taken, 2)
            pe.wait_ge(qx_pad, 2)
            pe.wait_ge(qx_ready, 1)
            for pair in range(2):
                parts_t(bank[2 + pair], 0, pair, qxt_ready)

            def scores(i, g):
                b, a = i // NG, i % NG
                for q in range(QT):
                    n = 2 * (GH * i + g) + q
                    behind = 4 if n < 2 * GH else 2
                    if n >= behind:
                        pe.wait_ge(max_done, n - behind + 1)
                    pe.matmul(score_bank(n)[:, :], qx_t[:, a, (2 * b + q) * P:(2 * b + q + 1) * P],
                              kx[:, a, g, b * SK:(b + 1) * SK], start=True, stop=True).then_inc(s_ready, 1)

            def turn_negmax(i):
                b, a = i // NG, i % NG
                pe.wait_ge(negmax_ready, i + 1)
                turn_begin(f"qm{i}")
                for q in range(QT):
                    mm = pe.transpose(turn[:, q * P:(q + 1) * P], qx[:, 2 * b + q, GH * a:GH * a + GH, :], ident)
                mm.then_inc(turn_full, 1)

            def scores_t(i, g):
                b, a = i // NG, i % NG
                n = GH * i + g
                pe.wait_ge(turn_free, full(f"qm{i}"))
                if n >= 2:
                    pe.wait_ge(exp_done, 2 * (n - 1))
                pair = 2 + 2 * (n % 2)
                for j in range(2):
                    pe.matmul(bank[pair + j][:, :], ident_b[:, :],
                              mbias_t[:, 2 * j:2 * j + 2, :].rearrange("p k q -> p (k q)"),
                              start=True, stop=False, skip_group_check=True)
                    for k in range(2):
                        at = b * SK + (2 * j + k) * P
                        mm = pe.matmul(bank[pair + j][:, k * S:(k + 1) * S], kx[:, a, g, at:at + P],
                                       qm_t[:, i % 2, :], start=False, stop=(k == 1), skip_group_check=True)
                mm.then_inc(st_ready, 1)

            def values(i):
                b, a = i // NG, i % NG
                pe.wait_ge(exp_done, 2 * GH * (i + 1))
                if i == 0:
                    pe.wait_ge(v_taken, 2)
                    pe.wait_ge(vx_pad, 3)
                    pe.wait_ge(pv_zero, 1)
                if i >= 1:
                    pe.wait_ge(pv_taken, i)
                for k in range(KT):
                    for g in range(GH):
                        mm = pe.matmul(bank[6][32 * g:32 * g + VROWS, 0:S], vx[:, b * KT + k, GH * a + g, :],
                                       pt[:, (GH * i + g) % (2 * GH), k * S:(k + 1) * S],
                                       start=(k == 0), stop=(k == KT - 1))
                mm.then_inc(pv_ready, 1)

            def turn_out(i):
                pe.wait_ge(pv_taken, i + 1)
                turn_begin(f"o{i}")
                for q in range(QT):
                    mm = pe.transpose(turn[:, q * P:(q + 1) * P], ot[:, i % 2, q * P:(q + 1) * P], ident)
                mm.then_inc(turn_full, 1)

            keep_clock(KEEP[6], bank[5])
            pe.wait_ge(v_taken, 1)
            pe.wait_ge(qxt_taken, 2)
            pe.wait_ge(in_ones, 16 * GH)
            pe.wait_ge(kx_rows, 16 * GH)
            for g in range(GH):
                scores(0, g)
                keep_clock(KEEP[7], turn)
            keep_clock(KEEP[8], turn)
            pe.wait_ge(identb_ready, 1)
            turn_negmax(0)
            for i in range(STEPS):
                for g in range(GH):
                    if i + 1 < STEPS:
                        if i + 1 == NG and g == 0:
                            pe.wait_ge(turn_free, full("qt3"))
                        scores(i + 1, g)
                    scores_t(i, g)
                    if (i, g) in inside:
                        issue(inside[i, g])
                    if (i, g) == (STEPS - 1, 1):
                        values(i - 1)
                if 1 <= i < STEPS - 1:
                    values(i - 1)
                if i + 1 < STEPS:
                    turn_negmax(i + 1)

            def up(u):
                b, e, hc = u // (EX * HC), u // HC % EX, u % HC
                if u >= 4:
                    pe.wait_ge(gelu_done, u - 3)
                if hc == 0 and b == 0:
                    pe.wait_ge(w1l_ready, e + 1)
                if u % (EX * HC) == 0:
                    pe.wait_ge(turn_free, full(f"x2_t{b}"))
                    pe.wait_ge(x2l_ready, b + 1)
                for k, (w, v) in enumerate(((w1h, x2h), (w1h, x2l), (w1l, x2h))):
                    mm = pe.matmul(bank[u % 4][:, 0:S], w[e][:, hc * P:(hc + 1) * P], v[:, b, :],
                                   start=(k == 0), stop=(k == 2))
                mm.then_inc(up_ready, 1)

            def down(u):
                b, e, hc = u // (EX * HC), u // HC % EX, u % HC
                o = u // HC
                pe.wait_ge(gelu_done, u + 1)
                if hc == 0 and o >= 2:
                    pe.wait_ge(acc_done, o - 1)
                for q in range(QT):
                    mm = pe.matmul(bank[4 + o % 2][:, q * P:(q + 1) * P], hs[:, u % 4, q * P:(q + 1) * P],
                                   w2s[:, e, hc, :], start=(hc == 0 and q == 0), stop=(hc == HC - 1),
                                   skip_group_check=True)
                mm.then_inc(down_done, 1)

            def turn_comb(b):
                pe.wait_ge(comb_ready, b + 1)
                turn_begin(f"comb_t{b}")
                for q in range(QT):
                    mm = pe.transpose(turn[0:EX, q * P:(q + 1) * P], comb[:, 2 * b + q, :], ident)
                mm.then_inc(turn_full, 1)

            def turn_b2(b):
                pe.wait_ge(turn_free, full(f"comb_t{b}"))
                turn_product(f"b2{b}", comb_t[0:EX, :], b2r[:, :], P)

            pe.wait_ge(max_done, 2 * GH * STEPS)
            for u in range(AHEAD):
                up(u)
            values(STEPS - 1)
            pe.wait_ge(in_w2, 16)
            pe.wait_ge(in_b2, 16)
            for u in range(UNITS):
                if u + AHEAD < UNITS:
                    up(u + AHEAD)
                down(u)
                if u == 1:
                    issue("o7")
                if u == 2:
                    turn_comb(0)
                if u == 4:
                    turn_b2(0)
                if u == 6:
                    issue("att2_t1")
                if u == 9:
                    issue("wo1")
                if u == 14:
                    issue("x2_t1")
                if u == 17:
                    issue("gate1")
                if u == 24:
                    turn_comb(1)
                if u == 27:
                    turn_b2(1)

        @block.vector
        def _(dve):
            chain = [0]

            def link(ins):
                chain[0] += 1
                ins.then_inc(v_chain, 1)
                dve.wait_ge(v_chain, chain[0])

            def note(ins):
                chain[0] += 1
                ins.then_inc(v_chain, 1)
                return chain[0]

            dve.memset(ident_b[:, :], 0.0).then_inc(warm_ready, 1)
            dve.memset(kx[:, 0, :, :].bitcast(F32), 0.0).then_inc(kx_zero_v, 1)
            dve.wait_ge(in_row, 16)
            in_b, rel = rw("in_b"), rw("rel").rearrange("p (r d) -> p r d", r=3)
            for s in range(B):
                dve.tensor_copy(bias_qkkv[:, s, 0:P], in_b[:, 0:P]).then_inc(v_chain, 1)
                dve.tensor_copy(bias_qkkv[:, s, 3 * P:4 * P], in_b[:, 2 * P:3 * P]).then_inc(v_chain, 1)
                for t in range(B):
                    dve.tensor_tensor(bias_qkkv[:, s, (1 + t) * P:(2 + t) * P].rearrange("p (h d) -> p h d", h=H),
                                      in_b[:, P:2 * P].rearrange("p (h d) -> p h d", h=H),
                                      rel[:, s - t + 1, :].unsqueeze(1).broadcast_to([P, H, D]),
                                      ALU.add).then_inc(v_chain, 1)
                chain[0] += 4
            dve.wait_ge(v_chain, chain[0])
            def sum_qkkv(t):
                dve.wait_ge(qkv_ready, t + 1)
                dve.tensor_tensor(qkkv[:, t, :], bank[t][:, :], bias_qkkv[:, t // QT, :], ALU.add)\
                    .then_inc(qkv_taken, 1)

            for t in range(NT):
                sum_qkkv(t)
            dve.wait_ge(qkv_taken, NT)

            def self_scores(t):
                for s in range(B):
                    dve.tensor_tensor(prod[:, t, s, :].rearrange("p (q n) -> p q n", q=QT),
                                      qkkv[:, 2 * t:2 * t + 2, 0:P],
                                      qkkv[:, 2 * s:2 * s + 2, (1 + t) * P:(2 + t) * P], ALU.mult).then_inc(v_chain, 1)
                chain[0] += 2
                dve.wait_ge(v_chain, chain[0])
                link(dve.tensor_reduce(sc[:, t, :, :].rearrange("p s n -> p (s n)"),
                                       prod[:, t, :, :].rearrange("p s (n d) -> p (s n) d", d=D), AX.X, ALU.add))
                link(dve.tensor_tensor(smax[:, t, :], sc[:, t, 0, :], sc[:, t, 1, :], ALU.max))
                dve.tensor_tensor(sd[:, t, :, :], sc[:, t, :, :],
                                  smax[:, t, :].unsqueeze(1).broadcast_to([P, B, QT * H]), ALU.subtract)\
                    .then_inc(sd_ready, 1)

            def self_probs(t):
                dve.wait_ge(se_ready, t + 1)
                link(dve.tensor_tensor(ssum[:, t, :], se[:, t, 0, :], se[:, t, 1, :], ALU.add))
                link(dve.reciprocal(srec[:, t, :], ssum[:, t, :]))
                dve.tensor_tensor(sp_[:, t, :, :], se[:, t, :, :],
                                  srec[:, t, :].unsqueeze(1).broadcast_to([P, B, QT * H]), ALU.mult)\
                    .then_inc(v_chain, 1)
                chain[0] += 1

            def self_values(t):
                dve.wait_ge(v_chain, chain[0])
                for s in range(B):
                    dve.tensor_tensor(prod[:, t, s, :].rearrange("p (q h d) -> p q h d", q=QT, h=H),
                                      qkkv[:, 2 * s:2 * s + 2, 3 * P:4 * P].rearrange("p q (h d) -> p q h d", h=H),
                                      sp_[:, t, s, :].rearrange("p (q h) -> p q h", q=QT).unsqueeze(3)
                                      .broadcast_to([P, QT, H, D]), ALU.mult).then_inc(v_chain, 1)
                chain[0] += 2
                dve.wait_ge(v_chain, chain[0])
                dve.tensor_tensor(att[:, 2 * t:2 * t + 2, :].rearrange("p q n -> p (q n)"),
                                  prod[:, t, 0, :], prod[:, t, 1, :], ALU.add).then_inc(att_ready, 1)

            self_scores(0)
            self_probs(0)
            self_values(0)
            dve.wait_ge(gone_ready, 1)
            link(dve.tensor_reduce(none_[:, :], gone[:, :, :], AX.X, ALU.min))
            link(dve.tensor_scalar(any_[:, :], none_[:, :], -1.0, 1.0, ALU.mult, ALU.add))
            dve.tensor_scalar(qsc[:, :], any_[:, :], HEAD_SCALE, None, ALU.mult).then_inc(v_chain, 1)
            dve.tensor_scalar(big[:, :], any_[:, :], NEG, None, ALU.mult).then_inc(v_chain, 1)
            chain[0] += 2
            dve.wait_ge(v_chain, chain[0])
            for q in range(QT):
                dve.tensor_scalar(mbias[:, q, :], gone[:, q, :], big[:, q:q + 1], None, ALU.mult)\
                    .then_inc(mbias_ready, 1)

            def context_values(b):
                dve.wait_ge(v_ready, b + 1)
                dve.tensor_tensor(vx[:, b * KT:(b + 1) * KT, :, 0:D],
                                  bank[6 * (1 - b)][:, :].rearrange("p (k h d) -> p k h d", k=KT, h=H),
                                  rw("bv").rearrange("p (h d) -> p h d", h=H).unsqueeze(1)
                                  .broadcast_to([P, KT, H, D]), ALU.add).then_inc(v_taken, 1)

            def norm(k, b, dst, done):
                for q in range(QT):
                    dve.bn_stats(stats[:, 2 * b + q, :], res[:, 2 * b + q, :]).then_inc(v_chain, 1)
                chain[0] += 2
                dve.wait_ge(v_chain, chain[0])
                for q in range(QT):
                    dve.bn_aggr(mv[:, 2 * b + q, :], stats[:, 2 * b + q, :]).then_inc(v_chain, 1)
                chain[0] += 2
                dve.wait_ge(v_chain, chain[0])
                dve.tensor_scalar(vare[:, 2 * b:2 * b + 2], mv[:, 2 * b:2 * b + 2, 1], LN_EPS, None, ALU.add)\
                    .then_inc(var_ready, 1)

            def norm_end(k, b, dst, done):
                dve.wait_ge(rstd_ready, k)
                for q in range(QT):
                    t = 2 * b + q
                    ins = dve.tensor_scalar(dst[:, t, :], res[:, t, :], mv[:, t, 0:1], rstd[:, t:t + 1],
                                            ALU.subtract, ALU.mult)
                    if q == 0:
                        ins.then_inc(v_chain, 1)
                        chain[0] += 1
                ins.then_inc(done, 1)

            def residual(b):
                dve.wait_ge(turn_full, full(f"out_w{b}"))
                dve.wait_ge(xb_ready, 1)
                dve.tensor_tensor(res[:, 2 * b:2 * b + 2, :], turn[:, 0:S].rearrange("p (q n) -> p q n", q=QT),
                                  xb[:, 2 * b:2 * b + 2, :], ALU.add).then_inc(turn_free, 1)

            def split_q(b):
                dve.wait_ge(turn_full, full(f"q{b}"))
                for q in range(QT):
                    ins = dve.scalar_tensor_tensor(qf[:, 2 * b + q, :], turn[:, q * P:(q + 1) * P], qsc[:, q:q + 1],
                                                   bqs[:, q, :], ALU.mult, ALU.add)
                    if q == 0:
                        ins.then_inc(v_chain, 1)
                        chain[0] += 1
                        dve.wait_ge(v_chain, chain[0])
                ins.then_inc(turn_free, 1)
                dve.wait_ge(turn_free, full(f"q{b}"))
                q_heads = qf[:, 2 * b:2 * b + 2, :].rearrange("p t (h d) -> p t h d", h=H)
                high, high2, low = [qx[:, 2 * b:2 * b + 2, :, 2:2 + 3 * D]
                                    .rearrange("p t h (d j) -> p t h d j", j=3)[:, :, :, :, j] for j in range(3)]
                dve.tensor_copy(high.bitcast(F32R), q_heads).then_inc(v_chain, 1)
                dve.tensor_copy(high2.bitcast(F32R), q_heads).then_inc(v_chain, 1)
                chain[0] += 2
                dve.wait_ge(v_chain, chain[0])
                dve.tensor_tensor(low.bitcast(F32R), q_heads, high, ALU.subtract).then_inc(qx_ready, 1)

            residual(0)
            dve.wait_ge(turn_free, full("out_w0"))
            norm(1, 0, x1, x1_ready)
            dve.wait_ge(in_col, 16)
            dve.tensor_copy(ident_b[:, :], ident).then_inc(identb_ready, 1)
            for q in range(QT):
                dve.tensor_scalar(bqs[:, q, :], rw("bq"), qsc[:, q:q + 1], None, ALU.mult).then_inc(v_chain, 1)
            chain[0] += 2
            context_values(1)
            norm_end(1, 0, x1, x1_ready)
            self_scores(1)
            split_q(0)
            self_probs(1)
            self_values(1)
            def row_max(i, g):
                b, a = i // NG, i % NG
                for q in range(QT):
                    n = 2 * (GH * i + g) + q
                    dve.wait_ge(s_ready, n + 1)
                    if n >= 4:
                        dve.wait_ge(max_done, n - 3)
                    h = GH * a + g
                    dve.tensor_tensor_reduce(junk[:, n % 4, :], score_bank(n)[:, :], mbias[:, q, :], 1.0, LOWEST,
                                             ALU.add, ALU.max, rowmax[:, 2 * b + q, h:h + 1]).then_inc(max_done, 1)

            def neg_max(i):
                b, a = i // NG, i % NG
                dve.wait_ge(max_done, 2 * GH * (i + 1))
                if i == 0:
                    dve.wait_ge(qxt_ready, 2)
                if i == NG:
                    dve.wait_ge(turn_full, full("qt3"))
                m = rowmax[:, 2 * b:2 * b + 2, GH * a:GH * a + GH]
                high = qx[:, 2 * b:2 * b + 2, GH * a:GH * a + GH, 0:1]
                low = qx[:, 2 * b:2 * b + 2, GH * a:GH * a + GH, 1:2]
                link(dve.tensor_scalar(high.bitcast(F32R), m.unsqueeze(3), -1.0, None, ALU.mult))
                for q in range(QT):
                    ins = dve.scalar_tensor_tensor(low[:, q].bitcast(F32R), m[:, q].unsqueeze(2), -1.0, high[:, q],
                                                   ALU.mult, ALU.subtract)
                    if q == 0:
                        ins.then_inc(v_chain, 1)
                        chain[0] += 1
                ins.then_inc(negmax_ready, 1)

            def take_negmax(i):
                dve.wait_ge(turn_full, full(f"qm{i}"))
                if i >= 2:
                    dve.wait_ge(st_ready, GH * (i - 1))
                dve.tensor_copy(qm_t[:, i % 2, :], turn[:, 0:S]).then_inc(turn_free, 1)

            def take_out(i):
                b, a = i // NG, i % NG
                dve.wait_ge(turn_full, full(f"o{i}"))
                o = turn[:, 0:S].rearrange("p (q g r) -> p q g r", q=QT, g=GH)
                link(dve.reciprocal(orec[:, :, :].unsqueeze(3), o[:, :, :, D:D + 1]))
                dst = att2[:, 2 * b:2 * b + 2, a * GH * D:(a + 1) * GH * D].rearrange("p q (g d) -> p q g d", g=GH)
                dve.tensor_tensor(dst, o[:, :, :, 0:D], orec[:, :, :].unsqueeze(3).broadcast_to([P, QT, GH, D]),
                                  ALU.mult).then_inc(turn_free, 1)

            def after_attention(b):
                dve.wait_ge(turn_full, full(f"wo{b}"))
                dve.wait_ge(x1b_ready, 1)
                dve.tensor_tensor(res[:, 2 * b:2 * b + 2, :], turn[:, 0:S].rearrange("p (q n) -> p q n", q=QT),
                                  x1b[:, 2 * b:2 * b + 2, :], ALU.add).then_inc(turn_free, 1)
                dve.wait_ge(turn_free, full(f"wo{b}"))
                norm(3 + b, b, x2, x2_ready)

            def x2_low(b):
                dve.wait_ge(x2t_ready, b + 1)
                dve.wait_ge(turn_free, full(f"x2_t{b}"))
                dve.tensor_tensor(x2l[:, b, :], x2_t[:, b, :], x2h[:, b, :].bitcast(F32), ALU.subtract)\
                    .then_inc(x2l_ready, 1)

            def router(b):
                two = slice(2 * b, 2 * b + 2)
                dve.wait_ge(turn_full, full(f"gate{b}"))
                dve.tensor_tensor(logit[:, two, :], turn[:, 0:S].rearrange("p (q n) -> p q n", q=QT)[:, :, 0:E],
                                  rw("gate_b").unsqueeze(1).broadcast_to([P, QT, E]), ALU.add).then_inc(turn_free, 1)
                dve.wait_ge(turn_free, full(f"gate{b}"))
                for t in range(2 * b, 2 * b + 2):
                    link(dve.max(top[:, t, :], logit[:, t, :]))
                    link(dve.max_index(topi[:, t, :], top[:, t, :], logit[:, t, :]))
                dve.tensor_copy(topf[:, two, :], topi[:, two, 0:2]).then_inc(v_chain, 1)
                chain[0] += 1
                dve.tensor_tensor(gap[:, two], top[:, two, 1], top[:, two, 0], ALU.subtract).then_inc(gap_ready, 1)

            def router_end(b):
                two = slice(2 * b, 2 * b + 2)
                dve.wait_ge(e2_ready, b + 1)
                link(dve.tensor_scalar(den[:, two], e2[:, two], 1.0, None, ALU.add))
                link(dve.reciprocal(gw[:, two, 0], den[:, two]))
                link(dve.tensor_tensor(gw[:, two, 1], e2[:, two], gw[:, two, 0], ALU.mult))
                for t in range(2 * b, 2 * b + 2):
                    link(dve.tensor_scalar(hot[:, t, :], rw("iota"), topf[:, t, 0:1], gw[:, t, 0:1],
                                           ALU.is_equal, ALU.mult))
                    link(dve.tensor_scalar(comb[:, t, 0:E], rw("iota"), topf[:, t, 1:2], gw[:, t, 1:2],
                                           ALU.is_equal, ALU.mult))
                    ins = dve.tensor_tensor(comb[:, t, 0:E], comb[:, t, 0:E], hot[:, t, :], ALU.add)
                    if t == 2 * b:
                        link(ins)
                ins.then_inc(comb_ready, 1)
                dve.wait_ge(comb_ready, b + 1)

            def acc_init(b):
                dve.wait_ge(turn_full, full(f"b2{b}"))
                dve.tensor_tensor(acc[:, 2 * b:2 * b + 2, :], turn[:, 0:S].rearrange("p (q n) -> p q n", q=QT),
                                  x2[:, 2 * b:2 * b + 2, :], ALU.add).then_inc(turn_free, 1)
                dve.wait_ge(turn_free, full(f"b2{b}"))

            def accumulate(o):
                b, e = o // EX, o % EX
                if o:
                    dve.wait_ge(acc_done, o)
                dve.wait_ge(down_done, HC * (o + 1))
                dst = res if e == EX - 1 else acc
                for q in range(QT):
                    t = 2 * b + q
                    ins = dve.scalar_tensor_tensor(dst[:, t, :], bank[4 + o % 2][:, q * P:(q + 1) * P],
                                                   comb[:, t, e:e + 1], acc[:, t, :], ALU.mult, ALU.add)
                    if q == 0:
                        link(ins)
                ins.then_inc(acc_done, 1)

            dve.wait_ge(mbias_ready, QT)
            for g in range(GH):
                row_max(0, g)
            neg_max(0)
            take_negmax(0)
            for i in range(STEPS):
                for g in range(GH):
                    if i + 1 < STEPS:
                        row_max(i + 1, g)
                    what = inside.get((i, g - 1), "")
                    if (i, g) == (1, 0):
                        context_values(0)
                        dve.wait_ge(v_taken, 2)
                        dve.memset(bank[6][:, 0:S], 0.0).then_inc(pv_zero, 1)
                    if what == "out_w1":
                        residual(1)
                        dve.wait_ge(turn_free, full("out_w1"))
                        norm(2, 1, x1, x1_ready)
                    if (i, g) == (1, 2):
                        norm_end(2, 1, x1, x1_ready)
                    if what == "q1":
                        split_q(1)
                    if what.startswith("o") and what[1:].isdigit():
                        take_out(int(what[1:]))
                    if what == "wo0":
                        after_attention(0)
                    if (i, g) == (7, 0):
                        norm_end(3, 0, x2, x2_ready)
                    if what == "gate0":
                        x2_low(0)
                        router(0)
                        router_end(0)
                if i + 1 < STEPS:
                    neg_max(i + 1)
                    take_negmax(i + 1)
            take_out(6)
            take_out(7)
            acc_init(0)
            accumulate(0)
            after_attention(1)
            accumulate(1)
            norm_end(4, 1, x2, x2_ready)
            accumulate(2)
            accumulate(3)
            x2_low(1)
            router(1)
            router_end(1)
            accumulate(4)
            accumulate(5)
            acc_init(1)
            for o in range(6, B * EX):
                accumulate(o)
                if o == EX - 1 or o == 2 * EX - 1:
                    b = o // EX
                    dve.wait_ge(acc_done, o + 1)
                    norm(5 + b, b, fin, fin_ready)
                    norm_end(5 + b, b, fin, fin_ready)


_OUT = ((B, S, P), "float32")


def kernel(**inputs):
    import numpy as np
    import concourse.bacc as bacc
    from concourse.bass_utils import run_bass_kernel_spmd

    def a(name):
        return np.asarray(inputs[name])

    x, c = a("x"), a("ctx_1024")
    w = a("L0_attn_in_proj_weight").T
    arrays = {
        "x_t_w": np.concatenate([x.reshape(B * S, P).T, w[:, 0:2 * P], w[:, P:3 * P]], axis=1),
        "x_tok": x.reshape(NT, P, P).transpose(1, 0, 2),
        "ctx_w": np.concatenate([c.reshape(B * SK, P).T, a("L0_xattn_wk").T, a("L0_xattn_wv").T], axis=1),
        "cols": np.concatenate([
            np.eye(P, dtype=np.float32), a("L0_attn_out_w").T, a("L0_xattn_wq").T, a("L0_xattn_wo").T,
            a("L0_ffn_gate_w"), a("L0_ffn_b1").reshape(E * HC, P).T, a("L0_ffn_bs1").reshape(HC, P).T,
            a("L0_xattn_bk").reshape(P, 1)], axis=1),
        "rows": np.concatenate([
            a("L0_attn_in_proj_bias"), a("L0_attn_rel_pos_keys")[REL - 1:REL + 2, 0:D].reshape(-1),
            a("L0_attn_out_b"), a("L0_xattn_bq"), a("L0_xattn_bv"), a("L0_xattn_bo"), a("L0_ffn_gate_b"),
            np.arange(E, dtype=np.float32), np.full(4, np.e, np.float32), np.full(4, -0.5, np.float32)])[None, :],
        "b2_rows": np.concatenate([a("L0_ffn_b2"), a("L0_ffn_bs2")[None, :]], axis=0),
        "mask": a("mask_1x1xSxS2_ik0").reshape(QT, P, SK).transpose(1, 0, 2),
        "w1": np.concatenate([a("L0_ffn_w1"), a("L0_ffn_ws1")[None]], axis=0).transpose(1, 0, 2),
        "w2": np.concatenate([a("L0_ffn_w2"), a("L0_ffn_ws2")[None]], axis=0)
              .reshape(EX, HC, P, P).transpose(2, 0, 1, 3),
    }
    arrays = {k: np.ascontiguousarray(v) for k, v in arrays.items()}
    nc = bacc.Bacc("TRN2", target_bir_lowering=False, num_devices=1)
    aps = {k: nc.dram_tensor(k, v.shape, mybir.dt.from_np(v.dtype), kind="ExternalInput").ap()
           for k, v in arrays.items()}
    aps["rows"] = aps["rows"].broadcast_to([P, ROW_N])
    y = nc.dram_tensor("y", _OUT[0], F32, kind="ExternalOutput").ap()
    heads = nc.dram_tensor("heads", (H, D, 3, B * SK), F32, kind="Internal").ap()
    decoder_layer(nc, *aps.values(), heads, y)
    r = run_bass_kernel_spmd(nc, [arrays], core_ids=[0])
    return r.results[0]["y"]
```

```python
from contextlib import ExitStack

import concourse.bass as bass
from concourse import mybir

F32 = mybir.dt.float32
F32R = mybir.dt.float32r
BF16 = mybir.dt.bfloat16
I32 = mybir.dt.int32
U32 = mybir.dt.uint32
ALU = mybir.AluOpType
ACT = mybir.ActivationFunctionType
AX = mybir.AxisListType

P = 128
B = 2
S = 256
SK = 512
H = 16
D = P // H
NT = B * S // P
QT = S // P
KT = SK // P
E = 8
EX = E + 1
HID = 512
HC = HID // P
GH = 4
NG = H // GH
QROWS = 32
KROWS = 2 + 3 * D
VROWS = 16
STEPS = B * NG
LN_EPS = 1e-5
HEAD_SCALE = float(D) ** -0.5
NEG = -1e9
LOWEST = -3.0e38
WARM = 20
KEEP = (8, 1, 2, 3, 1, 5, 2, 1, 3)
KEYS_FIRST = 3
SPLIT_FROM = 4
IN_STEPS = 15
AHEAD = 6
LAG = 4
REL = 16

PROJ_W = 4 * P
ROW = {}
_at = 0
for _name, _n in (("in_b", 3 * P), ("rel", 3 * D), ("out_b", P), ("bq", P), ("bv", P), ("bo", P),
                  ("gate_b", E), ("iota", E), ("e", 4), ("minus_half", 4)):
    ROW[_name] = (_at, _at + _n)
    _at += _n
ROW_N = _at
COL = {}
_at = 0
for _name, _n in (("ident", P), ("out_w", P), ("wq", P), ("wo", P), ("gate_w", E), ("b1", EX * HC), ("bk", 1)):
    COL[_name] = (_at, _at + _n)
    _at += _n
COL_N = _at


def decoder_layer(nc, x_t_w, x_tok, ctx_w, cols, rows, b2_rows, mask, w1, w2, heads, weights, out):
    with ExitStack() as ctx:
        def sb(name, shape, dt=F32):
            return ctx.enter_context(nc.sbuf_tensor(name, shape, dt))

        def sem(name):
            return ctx.enter_context(nc.semaphore(name))

        def views(region, *shapes):
            out, at = [], 0
            for shape in shapes:
                n = 1
                for k in shape:
                    n *= k
                v = region[:, at:at + n]
                names = "abcd"[:len(shape)]
                if len(shape) > 1:
                    v = v.rearrange(f"p ({' '.join(names)}) -> p {' '.join(names)}", **dict(zip(names, shape)))
                out.append(v)
                at += n
            assert at <= region.shape[1]
            return out

        region_p = sb("region_p", [P, 2 * GH * KT * S])
        region_m = sb("region_m", [P, QT * SK + B * PROJ_W])
        region_n = sb("region_n", [P, QT * SK])
        region_x = sb("region_x", [P, B * S + PROJ_W])
        region_j = sb("region_j", [P, 4 * SK // 2])
        region_b = sb("region_b", [P, NT * P])
        region_t = sb("region_t", [P, NT * P])
        [xw] = views(region_x, (B * S + PROJ_W,))
        kf, kh_, kl_, cw, qkkv, prod, xtok = views(
            region_p, (B * SK,), (B * SK,), (B * SK,), (B * SK + 2 * P,),
            (NT, PROJ_W), (B, B, QT * P),
            (NT, P))
        kh, kl = kh_.bitcast(F32R), kl_.bitcast(F32R)
        col = sb("col", [P, COL_N])
        row = sb("row", [P, ROW_N])
        b2r = sb("b2r", [EX, P])
        msk, bias_qkkv = views(region_m, (QT, SK), (B, PROJ_W))
        msk = msk.bitcast(I32)
        w1s = sb("w1s", [P, EX, HID])
        w2s = sb("w2s", [P, EX, HC, P])

        def rw(name):
            return row[:, ROW[name][0]:ROW[name][1]]

        def cl(name):
            return col[:, COL[name][0]:COL[name][1]]

        ident = cl("ident")
        sc = sb("sc", [P, B, B, QT * H])
        smax = sb("smax", [P, B, QT * H])
        sd = sb("sd", [P, B, B, QT * H])
        se = sb("se", [P, B, B, QT * H])
        ssum = sb("ssum", [P, B, QT * H])
        srec = sb("srec", [P, B, QT * H])
        sp_ = sb("sp_", [P, B, B, QT * H])
        [ones] = views(region_j, (B * SK,))
        att, att_t = views(region_x, (NT, P), (NT * P,))
        [xb] = views(region_b, (NT, P))
        res = sb("res", [P, NT, P])
        stats = sb("stats", [P, NT, 6])
        mv = sb("mv", [P, NT, 2])
        vare = sb("vare", [P, NT])
        rstd = sb("rstd", [P, NT])
        x1 = sb("x1", [P, NT, P])
        [x1b] = views(region_b, (NT, P))
        [x1_t] = views(region_t, (NT * P,))
        [gone] = views(region_n, (QT, SK))
        none_ = sb("none_", [P, QT])
        any_ = sb("any_", [P, QT])
        qsc = sb("qsc", [P, QT])
        big = sb("big", [P, QT])
        bqs = sb("bqs", [P, QT, P])
        mbias = sb("mbias", [P, QT, SK])
        mbias_t = sb("mbias_t", [P, KT, S], BF16)
        ident_b = sb("ident_b", [P, P], BF16)
        kx = sb("kx", [P, NG, GH, B * SK], F32R)
        vx = sb("vx", [P, B * KT, H, VROWS])
        qf = sb("qf", [P, NT, P])
        qx = sb("qx", [P, NT, H, QROWS])
        qx_t = sb("qx_t", [P, NG, NT * P], F32R)
        qm_t = sb("qm_t", [P, 2, S], F32R)
        junk = region_j[:, :].bitcast(BF16).rearrange("p (n k) -> p n k", n=4)
        rowmax = sb("rowmax", [P, NT, H])
        [pt] = views(region_p, (2 * GH, KT * S))
        orec = sb("orec", [P, QT, GH])
        att2, ot = views(region_x, (NT, P), (2, S))
        [att2_t, comb_t] = views(region_t, (S,), (S,))
        x2, x2_t = views(region_n, (NT, P), (B, S))
        logit = sb("logit", [P, NT, E])
        top = sb("top", [P, NT, 8])
        topi = sb("topi", [P, NT, 8], U32)
        topf = sb("topf", [P, NT, 2])
        gap = sb("gap", [P, NT])
        e2 = sb("e2", [P, NT])
        den = sb("den", [P, NT])
        gw = sb("gw", [P, NT, 2])
        hot = sb("hot", [P, NT, E])
        comb = sb("comb", [P, NT, EX])
        hs_first, acc, fin = views(region_m, (4, S), (B, S), (NT, P))

        spare = sb("spare", [P, HID], F32R)
        qx_flat = qx_t[:, :, :].rearrange("p a n -> p (a n)")
        x2h, x2l = [qx_flat[:, B * S * k:B * S * (k + 1)].rearrange("p (b n) -> p b n", b=B) for k in range(2)]
        [tmp] = views(region_j, (S,))
        h_high, h_low = [qx[:, 2 * k:2 * k + 2, :, :].bitcast(F32R).rearrange("p t h r -> p (t h r)")
                         .rearrange("p (u n) -> p u n", u=4) for k in range(2)]
        chunk = [kx[:, a, g, 0:HID] for a in range(NG) for g in range(GH)]
        chunk += [kx[:, a, g, SK:SK + HID] for a in range(NG - 1) for g in range(GH)]
        chunk += [qx_flat[:, (2 + k) * HID:(3 + k) * HID] for k in range(2)]
        chunk += [kx[:, NG - 1, g, SK:SK + HID] for g in range(GH)]
        chunk += [qm_t[:, :, :].rearrange("p k n -> p (k n)"), spare[:, :]]
        order = [E] + list(range(E))
        w_high, w_low = chunk[0::2], chunk[1::2]
        cb = pt[:, 0:4, :].rearrange("p s n -> p (s n)").rearrange("p (b e n) -> p b e n", b=B, e=E)
        hs_second = pt[:, 4, :].rearrange("p (u n) -> p u n", u=4)

        def hs(u):
            return (hs_first if u % 8 < 4 else hs_second)[:, u % 4, :]

        bank = [ctx.enter_context(nc.psum_tensor(f"bank{i}", [P, 512], F32)) for i in range(8)]
        turn = bank[7]

        in_bias, in_x_rest = sem("in_bias"), sem("in_x_rest")
        in_row, in_xw, in_cw, in_col = sem("in_row"), sem("in_xw"), sem("in_cw"), sem("in_col")
        in_x, in_mask, in_w1, in_w2, in_b2 = sem("in_x"), sem("in_mask"), sem("in_w1"), sem("in_w2"), sem("in_b2")
        ones_ready, in_ones, heads_done = sem("ones_ready"), sem("in_ones"), sem("heads_done")
        kx_rows, out_done = sem("kx_rows"), sem("out_done")
        qkv_ready, qkv_taken = sem("qkv_ready"), sem("qkv_taken")
        sd_ready, se_ready = sem("sd_ready"), sem("se_ready")
        gone_ready, qx_pad = sem("gone_ready"), sem("qx_pad")
        wh_ready, wl_ready, x2t_ready, x2l_ready = (
            sem("wh_ready"), sem("wl_ready"), sem("x2t_ready"), sem("x2l_ready"))
        comb_stored = sem("comb_stored")
        cb_ready = [sem(f"cb_ready{j}") for j in range(E // 2)]
        high_by_v, high_by_a, low_by_v, low_by_g = sem("high_by_v"), sem("high_by_a"), sem("low_by_v"), sem("low_by_g")
        mul_done = sem("mul_done")
        att_ready = sem("att_ready")
        var_ready, rstd_ready = sem("var_ready"), sem("rstd_ready")
        x1_ready, xb_ready, x1b_ready = sem("x1_ready"), sem("xb_ready"), sem("x1b_ready")
        kt_ready, kt_taken = sem("kt_ready"), sem("kt_taken")
        v_ready, v_taken = sem("v_ready"), sem("v_taken")
        kx_zero_v, kx_zero_g, kx_zero_a, vx_pad = sem("kx_zero_v"), sem("kx_zero_g"), sem("kx_zero_a"), sem("vx_pad")
        kl_ready, identb_ready = sem("kl_ready"), sem("identb_ready")
        mbias_ready, mt_ready, mt_taken = sem("mbias_ready"), sem("mt_ready"), sem("mt_taken")
        qx_ready, qxt_ready, qxt_taken = sem("qx_ready"), sem("qxt_ready"), sem("qxt_taken")
        turn_full, turn_free = sem("turn_full"), sem("turn_free")
        s_ready, max_done, negmax_ready = sem("s_ready"), sem("max_done"), sem("negmax_ready")
        st_ready, exp_done = sem("st_ready"), sem("exp_done")
        pv_ready, pv_taken, pv_zero = sem("pv_ready"), sem("pv_taken"), sem("pv_zero")
        x2_ready, comb_ready = sem("x2_ready"), sem("comb_ready")
        gap_ready, e2_ready = sem("gap_ready"), sem("e2_ready")
        up_ready, gelu_done, down_done, acc_done = sem("up_ready"), sem("gelu_done"), sem("down_done"), sem("acc_done")
        fin_ready = sem("fin_ready")
        warm_ready = sem("warm_ready")
        v_chain, g_chain = sem("v_chain"), sem("g_chain")

        inside = {(0, 0): "att_t1", (0, 1): "out_w1", (1, 1): "x1_t1", (1, 2): "q1", (2, 0): "qt2", (2, 1): "qt3",
                  (6, 0): "att2_t0", (6, 1): "wo0", (7, 0): "x2_t0", (7, 1): "gate0", (7, 3): "o6",
                  (6, 3): "o4"}
        for i in (2, 3, 4, 5, 7):
            inside[i, 2] = f"o{i - 2}"
        turns = ["att_t0", "out_w0", "x1_t0", "q0", "qm0"]
        for i in range(STEPS):
            turns += [inside[i, g] for g in range(GH) if (i, g) in inside]
            if i + 1 < STEPS:
                turns.append(f"qm{i + 1}")
        later = {1: "o7", 5: "att2_t1", 9: "wo1", 12: "b20", 16: "x2_t1", 20: "gate1", 27: "comb_t1",
                 41: "fin0", 48: "b21"}
        turns += ["comb_t0"] + [later[u] for u in sorted(later)] + ["fin1"]
        taken = {u + AHEAD - 1: what for u, what in later.items()}
        at = {what: u for u, what in taken.items()}
        turn_no = {what: k for k, what in enumerate(turns)}

        def full(what):
            return turn_no[what] + 1

        UNITS = B * EX * HC
        block = ctx.enter_context(nc.Block())

        def q_parts(b):
            parts = qx[:, 2 * b:2 * b + 2, :, 2:2 + 3 * D].rearrange("p t h (d j) -> p t h d j", j=3)
            return [qf[:, 2 * b:2 * b + 2, :].rearrange("p t (h d) -> p t h d", h=H)] + \
                [parts[:, :, :, :, j].bitcast(F32R) for j in range(3)]

        def score_bank(n):
            return bank[(0, 1, 4, 5)[n % 4]] if n < 2 * GH else bank[n % 2]

        @block.sync
        def _(sp):
            sp.dma_start(xw[:, 0:PROJ_W + P], x_t_w[:, 0:PROJ_W + P]).then_inc(in_xw, 16)
            sp.dma_start(xw[:, PROJ_W + P:], x_t_w[:, PROJ_W + P:]).then_inc(in_x_rest, 16)
            sp.dma_start(row[:, 0:ROW["out_b"][0]], rows[:, 0:ROW["out_b"][0]]).then_inc(in_bias, 16)
            sp.dma_start(cw[:, :], ctx_w).then_inc(in_cw, 16)
            sp.dma_start(row[:, ROW["out_b"][0]:], rows[:, ROW["out_b"][0]:]).then_inc(in_row, 16)
            sp.dma_start(col[:, :], cols).then_inc(in_col, 16)
            sp.dma_start(xtok[:, :, :], x_tok).then_inc(in_x, 16)
            sp.dma_start(msk[:, :, :], mask).then_inc(in_mask, 16)
            sp.wait_ge(ones_ready, 1)
            sp.wait_ge(kx_zero_v, 1)
            sp.wait_ge(kx_zero_a, 3)
            sp.wait_ge(kx_zero_g, 1)
            for g in range(GH):
                sp.dma_start(kx[32 * g:32 * g + 2, :, g, :].bitcast(F32),
                             ones[0:2, :].unsqueeze(1).broadcast_to([2, NG, B * SK])).then_inc(in_ones, 16)
            parts = heads.rearrange("h d j n -> (h d) j n")
            sp.wait_ge(kt_taken, 4)
            for j in (0, 2):
                sp.dma_start(parts[:, j, :], kh_[:, :]).then_inc(heads_done, 16)
            sp.wait_ge(kl_ready, 1)
            sp.dma_start(parts[:, 1, :], kl_[:, :]).then_inc(heads_done, 16)
            sp.wait_ge(heads_done, 16 * 3)
            for g in range(GH):
                sp.dma_start(kx[32 * g + 2:32 * g + KROWS, :, g, :].bitcast(F32),
                             heads.rearrange("(a g) d j n -> g (d j) a n", g=GH)[g]).then_inc(kx_rows, 16)
            sp.dma_start(w1s[:, :, :], w1).then_inc(in_w1, 16)
            sp.dma_start(b2r[:, :], b2_rows).then_inc(in_b2, 16)
            sp.dma_start(w2s[:, :, :, :], w2).then_inc(in_w2, 16)
            for b in range(B):
                sp.wait_ge(turn_free, full(f"comb_t{b}"))
                sp.dma_start(weights[b], comb_t[0:E, 0:S]).then_inc(comb_stored, 16)
                sp.wait_ge(comb_stored, 16 * (b + 1))
                sp.wait_ge(pv_ready, STEPS - 1)
                for e in range(0, E, 2):
                    if b:
                        sp.wait_ge(mul_done, e + 2)
                    sp.dma_start(cb[:, b, e:e + 2, :].rearrange("p e n -> p (e n)"),
                                 weights[b, e:e + 2, :].rearrange("e n -> (e n)").unsqueeze(0)
                                 .broadcast_to([P, 2 * S])).then_inc(cb_ready[e // 2], 16)
            for b in range(B):
                sp.wait_ge(fin_ready, b + 1)
                sp.dma_start(out[b].rearrange("(t p) d -> p t d", p=P), fin[:, 2 * b:2 * b + 2, :])\
                    .then_inc(out_done, 16)
            sp.wait_ge(out_done, 16 * B)

        @block.gpsimd
        def _(pool):
            pool.memset(ones[0:2, :], 1.0).then_inc(ones_ready, 1)
            pool.memset(kx[:, 2:4, :, :].bitcast(F32), 0.0).then_inc(kx_zero_g, 1)
            pool.wait_ge(in_row, 16)
            pool.wait_ge(in_x, 16)
            pool.tensor_tensor(xb[:, :, :], xtok[:, :, :], rw("out_b").unsqueeze(1).broadcast_to([P, NT, P]),
                               ALU.add).then_inc(xb_ready, 1)
            pool.wait_ge(in_mask, 16)
            pool.tensor_scalar(gone[:, :, :], msk[:, :, :], 0.0, None, ALU.is_equal).then_inc(gone_ready, 1)
            pool.wait_ge(kt_taken, 4)
            pool.tensor_tensor(kl[:, :], kf[:, :], kh[:, :].bitcast(F32), ALU.subtract).then_inc(kl_ready, 1)
            pool.memset(qx[:, :, :, 0:2], 0.0).then_inc(qx_pad, 1)
            pool.memset(qx[:, :, :, 2 + 3 * D:QROWS], 0.0).then_inc(qx_pad, 1)
            pool.memset(vx[:, :, :, D:D + 1], 1.0).then_inc(vx_pad, 1)
            pool.memset(vx[:, :, :, D + 1:VROWS], 0.0).then_inc(vx_pad, 1)
            pool.memset(comb[:, :, E:EX], 1.0).then_inc(vx_pad, 1)

            def inv_sqrt(k, t0):
                pool.wait_ge(var_ready, k)
                pool.tensor_tensor(rstd[:, t0:t0 + 2], vare[:, t0:t0 + 2], rw("minus_half")[:, 0:2], ALU.pow)\
                    .then_inc(rstd_ready, 1)

            def router_exp(b):
                pool.wait_ge(gap_ready, b + 1)
                pool.tensor_tensor(e2[:, 2 * b:2 * b + 2], rw("e")[:, 0:2], gap[:, 2 * b:2 * b + 2], ALU.pow)\
                    .then_inc(e2_ready, 1)

            def weights_low(m):
                pool.wait_ge(wh_ready, m + 1)
                src = w1s[:, order[m // 2], :] if m % 2 == 0 else \
                    w2s[:, order[m // 2], :, :].rearrange("p c n -> p (c n)")
                pool.tensor_tensor(w_low[m], src, w_high[m].bitcast(F32), ALU.subtract).then_inc(wl_ready, 1)

            inv_sqrt(1, 0)
            inv_sqrt(2, 2)
            pool.wait_ge(x1_ready, 2)
            pool.tensor_tensor(x1b[:, :, :], x1[:, :, :], rw("bo").unsqueeze(1).broadcast_to([P, NT, P]),
                               ALU.add).then_inc(x1b_ready, 1)
            q_heads, high, high2, low = q_parts(1)
            pool.wait_ge(turn_free, full("q1"))
            pool.tensor_copy(high, q_heads).then_inc(g_chain, 1)
            pool.tensor_copy(high2, q_heads).then_inc(g_chain, 1)
            pool.wait_ge(g_chain, 2)
            pool.tensor_tensor(low, q_heads, high.bitcast(F32), ALU.subtract).then_inc(qx_ready, 1)
            for m in range(IN_STEPS):
                weights_low(m)
                if m == 10:
                    inv_sqrt(3, 0)
                if m == 13:
                    router_exp(0)
            for u in range(UNITS):
                if u % 2 == 0:
                    pool.wait_ge(high_by_v, u // 2 + 1)
                    if u >= 4:
                        pool.wait_ge(down_done, u - 3)
                    pool.tensor_tensor(h_low[:, u % 4, :], hs(u), h_high[:, u % 4, :].bitcast(F32),
                                       ALU.subtract).then_inc(low_by_g, 1)
                if u == at["wo1"] + 1:
                    inv_sqrt(4, 2)
                if u in (13, 17, 21):
                    weights_low(15 + (u - 13) // 4)
                if u == at["gate1"]:
                    router_exp(1)
                if u == at["fin0"] + 1:
                    inv_sqrt(5, 0)
            inv_sqrt(6, 2)

        @block.scalar
        def _(act):

            act.wait_ge(kx_zero_v, 1)
            act.activation(kx[:, 1, 0:2, :], kx[:, 0, 0:2, :].bitcast(F32), ACT.Copy).then_inc(kx_zero_a, 1)
            act.activation(kx[:, 1, 2:4, :], kx[:, 0, 0:2, :].bitcast(F32), ACT.Copy).then_inc(kx_zero_a, 1)
            act.activation(kx[:, 0, 2:4, :], kx[:, 0, 0:2, :].bitcast(F32), ACT.Copy).then_inc(kx_zero_a, 1)
            act.wait_ge(in_col, 16)
            for b in range(B):
                act.wait_ge(kt_ready, b + 1)
                act.activation(kf[:, b * SK:(b + 1) * SK], bank[4 + b][:, :], ACT.Identity, bias=cl("bk"))\
                    .then_inc(kt_taken, 1)
                act.activation(kh[:, b * SK:(b + 1) * SK], bank[4 + b][:, :], ACT.Identity, bias=cl("bk"))\
                    .then_inc(kt_taken, 1)
            def self_exp(t):
                act.wait_ge(sd_ready, t + 1)
                act.activation(se[:, t, :, :], sd[:, t, :, :], ACT.Exp, scale=HEAD_SCALE).then_inc(se_ready, 1)

            def take(what, dst, src):
                act.wait_ge(turn_full, full(what))
                act.activation(dst, src, ACT.Copy).then_inc(turn_free, 1)

            def weights_high(m):
                src = w1s[:, order[m // 2], :] if m % 2 == 0 else \
                    w2s[:, order[m // 2], :, :].rearrange("p c n -> p (c n)")
                act.activation(w_high[m], src, ACT.Copy).then_inc(wh_ready, 1)

            def take_x2(b):
                act.wait_ge(turn_full, full(f"x2_t{b}"))
                act.activation(x2_t[:, b, :], turn[:, 0:S], ACT.Copy).then_inc(x2t_ready, 1)
                act.activation(x2h[:, b, :], turn[:, 0:S], ACT.Copy).then_inc(turn_free, 1)

            def unit_high(u):
                act.wait_ge(gelu_done, u + 1)
                if u >= 4:
                    act.wait_ge(down_done, u - 3)
                act.activation(h_high[:, u % 4, :], hs(u), ACT.Copy).then_inc(high_by_a, 1)

            def take_values(i):
                if i >= 2:
                    act.wait_ge(turn_full, full(f"o{i - 2}"))
                act.wait_ge(pv_ready, i + 1)
                act.activation(ot[:, i % 2, :], bank[6][:, 0:S], ACT.Copy).then_inc(pv_taken, 1)

            self_exp(0)
            take("att_t0", att_t[:, 0:S], turn[:, 0:S])
            for half in range(2):
                act.wait_ge(mt_ready, half + 1)
                act.activation(mbias_t[:, 2 * half:2 * half + 2, :].rearrange("p k q -> p (k q)"),
                               bank[1 + 2 * half][:, :], ACT.Copy).then_inc(mt_taken, 1)
            take("x1_t0", x1_t[:, 0:S], turn[:, 0:S])
            self_exp(1)
            for pair in range(2):
                act.wait_ge(qxt_ready, pair + 1)
                act.activation(qx_t[:, 2 * pair:2 * pair + 2, 0:S],
                               bank[2 + pair][:, :].rearrange("p (a q) -> p a q", a=2), ACT.Copy)\
                    .then_inc(qxt_taken, 1)
            for i in range(STEPS):
                for g in range(GH):
                    n = GH * i + g
                    act.wait_ge(st_ready, n + 1)
                    if i >= 2:
                        act.wait_ge(pv_ready, i - 1)
                    pair = 2 + 2 * (n % 2)
                    for j in range(2):
                        act.activation(pt[:, n % (2 * GH), 512 * j:512 * j + 512], bank[pair + j][:, :], ACT.Exp)\
                            .then_inc(exp_done, 1)
                    what = inside.get((i, g))
                    if what == "x2_t0":
                        take_x2(0)
                    if g == 0 and i >= 2:
                        take_values(i - 2)
                    if what == "att_t1":
                        take(what, att_t[:, S:2 * S], turn[:, 0:S])
                    if what == "x1_t1":
                        take(what, x1_t[:, S:2 * S], turn[:, 0:S])
                    if what in ("qt2", "qt3"):
                        pair = int(what[2]) - 2
                        take(what, qx_t[:, 2 * pair:2 * pair + 2, S:2 * S],
                             turn[:, :].rearrange("p (a q) -> p a q", a=2))
                    if what == "att2_t0":
                        take(what, att2_t[:, :], turn[:, 0:S])
                    m = GH * (i - SPLIT_FROM) + g
                    if m == 0:
                        act.wait_ge(in_w1, 16)
                        act.wait_ge(in_w2, 16)
                    if 0 <= m < IN_STEPS:
                        weights_high(m)
                    if (i, g) == (STEPS - 1, 2):
                        take_values(STEPS - 2)
            for u in range(UNITS):
                e, hc = order[u // HC % EX], u % HC
                act.wait_ge(up_ready, u + 1)
                if u >= 8:
                    act.wait_ge(low_by_v if u % 2 else low_by_g, (u - 8) // 2 + 1)
                act.activation(hs(u), bank[u % 4][:, 0:S], ACT.Gelu,
                               bias=col[:, COL["b1"][0] + e * HC + hc:COL["b1"][0] + e * HC + hc + 1])\
                    .then_inc(gelu_done, 1)
                if u % 2 == 0 and u:
                    unit_high(u - 1)
                if u == 1:
                    take_values(STEPS - 1)
                    take("comb_t0", comb_t[0:EX, :], turn[0:EX, 0:S])
                what = taken.get(u)
                if what == "att2_t1":
                    take(what, att2_t[:, :], turn[:, 0:S])
                if what == "x2_t1":
                    take_x2(1)
                if what == "comb_t1":
                    act.wait_ge(comb_stored, 16)
                    take(what, comb_t[0:EX, :], turn[0:EX, 0:S])
                if u in (11, 15, 19):
                    weights_high(15 + (u - 11) // 4)
            unit_high(UNITS - 1)

        @block.tensor
        def _(pe):
            def turn_begin(what):
                if turn_no[what]:
                    pe.wait_ge(turn_free, turn_no[what])

            pe.wait_ge(warm_ready, 1)
            for k in range(WARM):
                pe.matmul(turn[:, 0:P], ident_b[:, :], ident_b[:, :], start=True, stop=True)

            def keep_clock(n, into):
                for k in range(n):
                    pe.matmul(into[:, 0:P], ident, ident, start=True, stop=True)

            pe.wait_ge(in_xw, 16)
            for t in range(NT):
                if t == 1:
                    pe.wait_ge(in_x_rest, 16)
                pe.matmul(bank[t][:, :], xw[:, PROJ_W + t * P:PROJ_W + (t + 1) * P], xw[:, 0:PROJ_W],
                          start=True, stop=True).then_inc(qkv_ready, 1)
            pe.wait_ge(in_cw, 16)
            for b in range(B):
                pe.matmul(bank[4 + b][:, :], cw[:, B * SK:B * SK + P], cw[:, b * SK:(b + 1) * SK],
                          start=True, stop=True).then_inc(kt_ready, 1)
            for b in range(B):
                if b == 1:
                    pe.wait_ge(qkv_taken, 1)
                for k in range(KT):
                    mm = pe.matmul(bank[6 * (1 - b)][:, k * P:(k + 1) * P],
                                   cw[:, (b * KT + k) * P:(b * KT + k + 1) * P],
                                   cw[:, B * SK + P:B * SK + 2 * P], start=True, stop=True)
                mm.then_inc(v_ready, 1)

            def masks_t():
                pe.wait_ge(mbias_ready, QT)
                pe.wait_ge(qkv_taken, NT)
                for half in range(2):
                    for k in range(2):
                        for q in range(QT):
                            kt = 2 * half + k
                            mm = pe.transpose(bank[1 + 2 * half][:, (k * QT + q) * P:(k * QT + q + 1) * P],
                                              mbias[:, q, kt * P:(kt + 1) * P], ident)
                    mm.then_inc(mt_ready, 1)

            def turn_tiles(what, src, b):
                turn_begin(what)
                for q in range(QT):
                    mm = pe.transpose(turn[:, q * P:(q + 1) * P], src[:, 2 * b + q, :], ident)
                mm.then_inc(turn_full, 1)

            def turn_product(what, lhs, rhs, n):
                turn_begin(what)
                for q in range(QT):
                    mm = pe.matmul(turn[:, q * P:q * P + n], lhs[:, q * P:(q + 1) * P], rhs, start=True, stop=True)
                mm.then_inc(turn_full, 1)

            def parts_t(dst, b, pair, done):
                for a2 in range(2):
                    for q in range(QT):
                        a = 2 * pair + a2
                        mm = pe.transpose(dst[:, (a2 * QT + q) * P:(a2 * QT + q + 1) * P],
                                          qx[:, 2 * b + q, GH * a:GH * a + GH, :], ident)
                mm.then_inc(done, 1)

            def issue(what):
                b = int(what[-1])
                if what.startswith("att_t"):
                    pe.wait_ge(att_ready, b + 1)
                    turn_tiles(what, att, b)
                elif what.startswith("out_w"):
                    pe.wait_ge(turn_free, full(f"att_t{b}"))
                    turn_product(what, att_t[:, b * S:(b + 1) * S], cl("out_w"), P)
                elif what.startswith("x1_t"):
                    pe.wait_ge(x1_ready, b + 1)
                    turn_tiles(what, x1, b)
                elif what.startswith("qt"):
                    pe.wait_ge(qx_ready, 2)
                    turn_begin(what)
                    parts_t(turn, 1, b - 2, turn_full)
                elif what.startswith("q"):
                    pe.wait_ge(turn_free, full(f"x1_t{b}"))
                    turn_product(what, x1_t[:, b * S:(b + 1) * S], cl("wq"), P)
                elif what.startswith("o"):
                    turn_out(b)
                elif what.startswith("att2_t"):
                    pe.wait_ge(turn_free, full(f"o{NG * (b + 1) - 1}"))
                    turn_tiles(what, att2, b)
                elif what.startswith("wo"):
                    pe.wait_ge(turn_free, full(f"att2_t{b}"))
                    turn_product(what, att2_t[:, :], cl("wo"), P)
                elif what.startswith("x2_t"):
                    pe.wait_ge(x2_ready, b + 1)
                    turn_tiles(what, x2, b)
                elif what.startswith("gate"):
                    pe.wait_ge(turn_free, full(f"x2_t{b}"))
                    turn_product(what, x2_t[:, b, :], cl("gate_w"), E)

            pe.wait_ge(in_col, 16)
            keep_clock(KEEP[0], turn)
            issue("att_t0")
            pe.wait_ge(kt_taken, 4)
            keep_clock(KEEP[1], bank[5])
            issue("out_w0")
            keep_clock(KEEP[2], bank[5])
            masks_t()
            keep_clock(KEEP[3], bank[5])
            issue("x1_t0")
            keep_clock(KEEP[4], bank[5])
            issue("q0")
            keep_clock(KEEP[5], bank[5])
            pe.wait_ge(mt_taken, 2)
            pe.wait_ge(qx_pad, 2)
            pe.wait_ge(qx_ready, 1)
            for pair in range(2):
                parts_t(bank[2 + pair], 0, pair, qxt_ready)

            def scores(i, g):
                b, a = i // NG, i % NG
                for q in range(QT):
                    n = 2 * (GH * i + g) + q
                    behind = 4 if n < 2 * GH else 2
                    if n >= behind:
                        pe.wait_ge(max_done, n - behind + 1)
                    pe.matmul(score_bank(n)[:, :], qx_t[:, a, (2 * b + q) * P:(2 * b + q + 1) * P],
                              kx[:, a, g, b * SK:(b + 1) * SK], start=True, stop=True).then_inc(s_ready, 1)

            def turn_negmax(i):
                b, a = i // NG, i % NG
                pe.wait_ge(negmax_ready, i + 1)
                turn_begin(f"qm{i}")
                for q in range(QT):
                    mm = pe.transpose(turn[:, q * P:(q + 1) * P], qx[:, 2 * b + q, GH * a:GH * a + GH, :], ident)
                mm.then_inc(turn_full, 1)

            def scores_t(i, g):
                b, a = i // NG, i % NG
                n = GH * i + g
                pe.wait_ge(turn_free, full(f"qm{i}"))
                if n >= 2:
                    pe.wait_ge(exp_done, 2 * (n - 1))
                pair = 2 + 2 * (n % 2)
                for j in range(2):
                    pe.matmul(bank[pair + j][:, :], ident_b[:, :],
                              mbias_t[:, 2 * j:2 * j + 2, :].rearrange("p k q -> p (k q)"),
                              start=True, stop=False, skip_group_check=True)
                    for k in range(2):
                        at = b * SK + (2 * j + k) * P
                        mm = pe.matmul(bank[pair + j][:, k * S:(k + 1) * S], kx[:, a, g, at:at + P],
                                       qm_t[:, i % 2, :], start=False, stop=(k == 1), skip_group_check=True)
                mm.then_inc(st_ready, 1)

            def values(i, first, end):
                b, a = i // NG, i % NG
                pe.wait_ge(exp_done, 2 * GH * (i + 1))
                if i == 0:
                    pe.wait_ge(v_taken, 2)
                    pe.wait_ge(vx_pad, 3)
                    pe.wait_ge(pv_zero, 1)
                if i >= 1:
                    pe.wait_ge(pv_taken, i)
                for k in range(first, end):
                    for g in range(GH):
                        mm = pe.matmul(bank[6][32 * g:32 * g + VROWS, 0:S], vx[:, b * KT + k, GH * a + g, :],
                                       pt[:, (GH * i + g) % (2 * GH), k * S:(k + 1) * S],
                                       start=(k == 0), stop=(k == KT - 1))
                if end == KT:
                    mm.then_inc(pv_ready, 1)

            def turn_out(i):
                pe.wait_ge(pv_taken, i + 1)
                turn_begin(f"o{i}")
                for q in range(QT):
                    mm = pe.transpose(turn[:, q * P:(q + 1) * P], ot[:, i % 2, q * P:(q + 1) * P], ident)
                mm.then_inc(turn_full, 1)

            keep_clock(KEEP[6], bank[5])
            pe.wait_ge(v_taken, 1)
            pe.wait_ge(qxt_taken, 2)
            pe.wait_ge(in_ones, 16 * GH)
            pe.wait_ge(kx_rows, 16 * GH)
            for g in range(GH):
                scores(0, g)
                keep_clock(KEEP[7], turn)
            keep_clock(KEEP[8], turn)
            pe.wait_ge(identb_ready, 1)
            turn_negmax(0)
            for i in range(STEPS):
                for g in range(GH):
                    if i + 1 < STEPS:
                        if i + 1 == NG and g == 0:
                            pe.wait_ge(turn_free, full("qt2"))
                        if i + 1 == NG + 2 and g == 0:
                            pe.wait_ge(turn_free, full("qt3"))
                        scores(i + 1, g)
                    if g == 0 and i >= 2:
                        values(i - 2, KEYS_FIRST, KT)
                    scores_t(i, g)
                    if (i, g) in inside:
                        issue(inside[i, g])
                    if (i, g) == (STEPS - 1, 2):
                        values(i - 1, 0, KT)
                if 1 <= i < STEPS - 1:
                    values(i - 1, 0, KEYS_FIRST)
                if i + 1 < STEPS:
                    turn_negmax(i + 1)

            def up(u):
                b, o, hc = u // (EX * HC), u // HC % EX, u % HC
                if u >= 4:
                    pe.wait_ge(gelu_done, u - 3)
                if hc == 0 and b == 0:
                    pe.wait_ge(wl_ready, 2 * o + 1)
                if u % (EX * HC) == 0:
                    pe.wait_ge(turn_free, full(f"x2_t{b}"))
                    pe.wait_ge(x2l_ready, b + 1)
                w = slice(hc * P, (hc + 1) * P)
                for k, (lhs, rhs) in enumerate(((w_high, x2h), (w_high, x2l), (w_low, x2h))):
                    mm = pe.matmul(bank[u % 4][:, 0:S], lhs[2 * o][:, w], rhs[:, b, :], start=(k == 0), stop=(k == 2))
                mm.then_inc(up_ready, 1)

            def down(u):
                b, o, hc = u // (EX * HC), u // HC % EX, u % HC
                n = u // HC
                if hc == 0 and b == 0:
                    pe.wait_ge(wl_ready, 2 * o + 2)
                if hc == 0 and n >= 3:
                    pe.wait_ge(mul_done, n - 2)
                if n == 2 and hc == 0:
                    pe.wait_ge(pv_taken, STEPS)
                pe.wait_ge(high_by_a if u % 2 else high_by_v, u // 2 + 1)
                w = slice(hc * P, (hc + 1) * P)
                for k, (lhs, rhs) in enumerate(((w_high, h_high), (w_low, h_high), (w_high, h_low))):
                    if k == 2:
                        pe.wait_ge(low_by_v if u % 2 else low_by_g, u // 2 + 1)
                    mm = pe.matmul(bank[4 + n % 3][:, 0:S], lhs[2 * o + 1][:, w], rhs[:, u % 4, :],
                                   start=(hc == 0 and k == 0), stop=(hc == HC - 1 and k == 2))
                mm.then_inc(down_done, 1)

            def turn_comb(b):
                pe.wait_ge(comb_ready, b + 1)
                turn_begin(f"comb_t{b}")
                for q in range(QT):
                    mm = pe.transpose(turn[0:EX, q * P:(q + 1) * P], comb[:, 2 * b + q, :], ident)
                mm.then_inc(turn_full, 1)

            def turn_b2(b):
                pe.wait_ge(turn_free, full(f"comb_t{b}"))
                turn_begin(f"b2{b}")
                pe.matmul(turn[:, 0:S], b2r[:, :], comb_t[0:EX, :], start=True, stop=True).then_inc(turn_full, 1)

            def turn_fin(b):
                pe.wait_ge(acc_done, EX * (b + 1))
                turn_begin(f"fin{b}")
                for q in range(QT):
                    mm = pe.transpose(turn[:, q * P:(q + 1) * P], acc[:, b, q * P:(q + 1) * P], ident)
                mm.then_inc(turn_full, 1)

            pe.wait_ge(max_done, 2 * GH * STEPS)
            pe.wait_ge(in_b2, 16)
            for u in range(3):
                up(u)
            values(STEPS - 1, 0, KT)
            turn_comb(0)
            for u in range(3, AHEAD):
                up(u)
            for u in range(UNITS):
                down(u)
                what = later.get(u, "")
                if what.startswith("comb_t"):
                    turn_comb(1)
                elif what.startswith("b2"):
                    turn_b2(int(what[-1]))
                elif what.startswith("fin"):
                    turn_fin(0)
                elif what:
                    issue(what)
                if u + AHEAD < UNITS:
                    up(u + AHEAD)
            turn_fin(1)

        @block.vector
        def _(dve):
            chain = [0]

            def link(ins):
                chain[0] += 1
                ins.then_inc(v_chain, 1)
                dve.wait_ge(v_chain, chain[0])

            def note(ins):
                chain[0] += 1
                ins.then_inc(v_chain, 1)
                return chain[0]

            dve.memset(ident_b[:, :], 0.0).then_inc(warm_ready, 1)
            dve.memset(kx[:, 0, 0:2, :].bitcast(F32), 0.0).then_inc(kx_zero_v, 1)
            dve.wait_ge(in_bias, 16)
            in_b, rel = rw("in_b"), rw("rel").rearrange("p (r d) -> p r d", r=3)
            for part, at_ in ((0, 0), (3, 2)):
                dve.tensor_copy(bias_qkkv[:, :, part * P:(part + 1) * P],
                                in_b[:, at_ * P:(at_ + 1) * P].unsqueeze(1).broadcast_to([P, B, P]))\
                    .then_inc(v_chain, 1)
            for t in range(B):
                dve.tensor_tensor(bias_qkkv[:, :, (1 + t) * P:(2 + t) * P].rearrange("p s (h d) -> p s h d", h=H),
                                  in_b[:, P:2 * P].rearrange("p (h d) -> p h d", h=H).unsqueeze(1)
                                  .broadcast_to([P, B, H, D]),
                                  rel[:, 1 - t:3 - t, :].unsqueeze(2).broadcast_to([P, B, H, D]),
                                  ALU.add).then_inc(v_chain, 1)
            chain[0] += 4
            dve.wait_ge(v_chain, chain[0])
            def sum_qkkv(t):
                dve.wait_ge(qkv_ready, t + 1)
                dve.tensor_tensor(qkkv[:, t, :], bank[t][:, :], bias_qkkv[:, t // QT, :], ALU.add)\
                    .then_inc(qkv_taken, 1)

            for t in range(NT):
                sum_qkkv(t)
            dve.wait_ge(qkv_taken, NT)

            def self_scores(t):
                for s in range(B):
                    dve.tensor_tensor(prod[:, t, s, :].rearrange("p (q n) -> p q n", q=QT),
                                      qkkv[:, 2 * t:2 * t + 2, 0:P],
                                      qkkv[:, 2 * s:2 * s + 2, (1 + t) * P:(2 + t) * P], ALU.mult).then_inc(v_chain, 1)
                chain[0] += 2
                dve.wait_ge(v_chain, chain[0])
                link(dve.tensor_reduce(sc[:, t, :, :].rearrange("p s n -> p (s n)"),
                                       prod[:, t, :, :].rearrange("p s (n d) -> p (s n) d", d=D), AX.X, ALU.add))
                link(dve.tensor_tensor(smax[:, t, :], sc[:, t, 0, :], sc[:, t, 1, :], ALU.max))
                dve.tensor_tensor(sd[:, t, :, :], sc[:, t, :, :],
                                  smax[:, t, :].unsqueeze(1).broadcast_to([P, B, QT * H]), ALU.subtract)\
                    .then_inc(sd_ready, 1)

            def self_probs(t):
                dve.wait_ge(se_ready, t + 1)
                link(dve.tensor_tensor(ssum[:, t, :], se[:, t, 0, :], se[:, t, 1, :], ALU.add))
                link(dve.reciprocal(srec[:, t, :], ssum[:, t, :]))
                dve.tensor_tensor(sp_[:, t, :, :], se[:, t, :, :],
                                  srec[:, t, :].unsqueeze(1).broadcast_to([P, B, QT * H]), ALU.mult)\
                    .then_inc(v_chain, 1)
                chain[0] += 1

            def self_values(t):
                dve.wait_ge(v_chain, chain[0])
                for s in range(B):
                    dve.tensor_tensor(prod[:, t, s, :].rearrange("p (q h d) -> p q h d", q=QT, h=H),
                                      qkkv[:, 2 * s:2 * s + 2, 3 * P:4 * P].rearrange("p q (h d) -> p q h d", h=H),
                                      sp_[:, t, s, :].rearrange("p (q h) -> p q h", q=QT).unsqueeze(3)
                                      .broadcast_to([P, QT, H, D]), ALU.mult).then_inc(v_chain, 1)
                chain[0] += 2
                dve.wait_ge(v_chain, chain[0])
                dve.tensor_tensor(att[:, 2 * t:2 * t + 2, :].rearrange("p q n -> p (q n)"),
                                  prod[:, t, 0, :], prod[:, t, 1, :], ALU.add).then_inc(att_ready, 1)

            self_scores(0)
            self_probs(0)
            self_values(0)
            dve.wait_ge(gone_ready, 1)
            link(dve.tensor_reduce(none_[:, :], gone[:, :, :], AX.X, ALU.min))
            link(dve.tensor_scalar(any_[:, :], none_[:, :], -1.0, 1.0, ALU.mult, ALU.add))
            dve.tensor_scalar(qsc[:, :], any_[:, :], HEAD_SCALE, None, ALU.mult).then_inc(v_chain, 1)
            dve.tensor_scalar(big[:, :], any_[:, :], NEG, None, ALU.mult).then_inc(v_chain, 1)
            chain[0] += 2
            dve.wait_ge(v_chain, chain[0])
            for q in range(QT):
                dve.tensor_scalar(mbias[:, q, :], gone[:, q, :], big[:, q:q + 1], None, ALU.mult)\
                    .then_inc(mbias_ready, 1)

            def context_values(b):
                dve.wait_ge(v_ready, b + 1)
                dve.tensor_tensor(vx[:, b * KT:(b + 1) * KT, :, 0:D],
                                  bank[6 * (1 - b)][:, :].rearrange("p (k h d) -> p k h d", k=KT, h=H),
                                  rw("bv").rearrange("p (h d) -> p h d", h=H).unsqueeze(1)
                                  .broadcast_to([P, KT, H, D]), ALU.add).then_inc(v_taken, 1)

            def norm(k, b, dst, done, src=None):
                for q in range(QT):
                    dve.bn_stats(stats[:, 2 * b + q, :], src[:, q, :] if src is not None else res[:, 2 * b + q, :]).then_inc(v_chain, 1)
                chain[0] += 2
                dve.wait_ge(v_chain, chain[0])
                for q in range(QT):
                    dve.bn_aggr(mv[:, 2 * b + q, :], stats[:, 2 * b + q, :]).then_inc(v_chain, 1)
                chain[0] += 2
                dve.wait_ge(v_chain, chain[0])
                dve.tensor_scalar(vare[:, 2 * b:2 * b + 2], mv[:, 2 * b:2 * b + 2, 1], LN_EPS, None, ALU.add)\
                    .then_inc(var_ready, 1)

            def norm_end(k, b, dst, done, src=None):
                dve.wait_ge(rstd_ready, k)
                for q in range(QT):
                    t = 2 * b + q
                    ins = dve.tensor_scalar(dst[:, t, :], src[:, q, :] if src is not None else res[:, t, :], mv[:, t, 0:1], rstd[:, t:t + 1],
                                            ALU.subtract, ALU.mult)
                    if q == 0:
                        ins.then_inc(v_chain, 1)
                        chain[0] += 1
                ins.then_inc(done, 1)

            def residual(b):
                dve.wait_ge(turn_full, full(f"out_w{b}"))
                dve.wait_ge(xb_ready, 1)
                dve.tensor_tensor(res[:, 2 * b:2 * b + 2, :], turn[:, 0:S].rearrange("p (q n) -> p q n", q=QT),
                                  xb[:, 2 * b:2 * b + 2, :], ALU.add).then_inc(turn_free, 1)

            def split_q(b):
                dve.wait_ge(turn_full, full(f"q{b}"))
                for q in range(QT):
                    ins = dve.scalar_tensor_tensor(qf[:, 2 * b + q, :], turn[:, q * P:(q + 1) * P], qsc[:, q:q + 1],
                                                   bqs[:, q, :], ALU.mult, ALU.add)
                    if q == 0:
                        ins.then_inc(v_chain, 1)
                        chain[0] += 1
                        dve.wait_ge(v_chain, chain[0])
                ins.then_inc(turn_free, 1)
                dve.wait_ge(turn_free, full(f"q{b}"))
                if b:
                    return
                q_heads, high, high2, low = q_parts(b)
                dve.tensor_copy(high, q_heads).then_inc(v_chain, 1)
                dve.tensor_copy(high2, q_heads).then_inc(v_chain, 1)
                chain[0] += 2
                dve.wait_ge(v_chain, chain[0])
                dve.tensor_tensor(low, q_heads, high.bitcast(F32), ALU.subtract).then_inc(qx_ready, 1)

            residual(0)
            dve.wait_ge(turn_free, full("out_w0"))
            norm(1, 0, x1, x1_ready)
            dve.wait_ge(in_col, 16)
            dve.tensor_copy(ident_b[:, :], ident).then_inc(identb_ready, 1)
            for q in range(QT):
                if q == 0:
                    dve.wait_ge(in_row, 16)
                dve.tensor_scalar(bqs[:, q, :], rw("bq"), qsc[:, q:q + 1], None, ALU.mult).then_inc(v_chain, 1)
            chain[0] += 2
            context_values(1)
            norm_end(1, 0, x1, x1_ready)
            self_scores(1)
            split_q(0)
            self_probs(1)
            self_values(1)
            context_values(0)
            def row_max(i, g):
                b, a = i // NG, i % NG
                for q in range(QT):
                    n = 2 * (GH * i + g) + q
                    dve.wait_ge(s_ready, n + 1)
                    if n >= 4:
                        dve.wait_ge(max_done, n - 3)
                    h = GH * a + g
                    dve.tensor_tensor_reduce(junk[:, n % 4, :], score_bank(n)[:, :], mbias[:, q, :], 1.0, LOWEST,
                                             ALU.add, ALU.max, rowmax[:, 2 * b + q, h:h + 1]).then_inc(max_done, 1)

            def neg_max(i):
                b, a = i // NG, i % NG
                dve.wait_ge(max_done, 2 * GH * (i + 1))
                if i == 0:
                    dve.wait_ge(qxt_ready, 2)
                if i == NG:
                    dve.wait_ge(turn_full, full("qt3"))
                m = rowmax[:, 2 * b:2 * b + 2, GH * a:GH * a + GH]
                high = qx[:, 2 * b:2 * b + 2, GH * a:GH * a + GH, 0:1]
                low = qx[:, 2 * b:2 * b + 2, GH * a:GH * a + GH, 1:2]
                link(dve.tensor_scalar(high.bitcast(F32R), m.unsqueeze(3), -1.0, None, ALU.mult))
                for q in range(QT):
                    ins = dve.scalar_tensor_tensor(low[:, q].bitcast(F32R), m[:, q].unsqueeze(2), -1.0, high[:, q],
                                                   ALU.mult, ALU.subtract)
                    if q == 0:
                        ins.then_inc(v_chain, 1)
                        chain[0] += 1
                ins.then_inc(negmax_ready, 1)

            def take_negmax(i):
                dve.wait_ge(turn_full, full(f"qm{i}"))
                if i >= 2:
                    dve.wait_ge(st_ready, GH * (i - 1))
                dve.tensor_copy(qm_t[:, i % 2, :], turn[:, 0:S]).then_inc(turn_free, 1)

            def take_out(i):
                b, a = i // NG, i % NG
                dve.wait_ge(turn_full, full(f"o{i}"))
                o = turn[:, 0:S].rearrange("p (q g r) -> p q g r", q=QT, g=GH)
                link(dve.reciprocal(orec[:, :, :].unsqueeze(3), o[:, :, :, D:D + 1]))
                dst = att2[:, 2 * b:2 * b + 2, a * GH * D:(a + 1) * GH * D].rearrange("p q (g d) -> p q g d", g=GH)
                dve.tensor_tensor(dst, o[:, :, :, 0:D], orec[:, :, :].unsqueeze(3).broadcast_to([P, QT, GH, D]),
                                  ALU.mult).then_inc(turn_free, 1)

            def after_attention(b):
                dve.wait_ge(turn_full, full(f"wo{b}"))
                dve.wait_ge(x1b_ready, 1)
                dve.tensor_tensor(res[:, 2 * b:2 * b + 2, :], turn[:, 0:S].rearrange("p (q n) -> p q n", q=QT),
                                  x1b[:, 2 * b:2 * b + 2, :], ALU.add).then_inc(turn_free, 1)
                dve.wait_ge(turn_free, full(f"wo{b}"))
                norm(3 + b, b, x2, x2_ready)

            def x2_low(b):
                dve.wait_ge(x2t_ready, b + 1)
                dve.wait_ge(turn_free, full(f"x2_t{b}"))
                dve.tensor_tensor(x2l[:, b, :], x2_t[:, b, :], x2h[:, b, :].bitcast(F32), ALU.subtract)\
                    .then_inc(x2l_ready, 1)

            def both(step, b):
                for t in range(2 * b, 2 * b + 2):
                    step(t).then_inc(v_chain, 1)
                chain[0] += 2
                dve.wait_ge(v_chain, chain[0])

            def router(b):
                two = slice(2 * b, 2 * b + 2)
                dve.wait_ge(turn_full, full(f"gate{b}"))
                dve.tensor_tensor(logit[:, two, :], turn[:, 0:S].rearrange("p (q n) -> p q n", q=QT)[:, :, 0:E],
                                  rw("gate_b").unsqueeze(1).broadcast_to([P, QT, E]), ALU.add).then_inc(turn_free, 1)
                dve.wait_ge(turn_free, full(f"gate{b}"))
                both(lambda t: dve.max(top[:, t, :], logit[:, t, :]), b)
                both(lambda t: dve.max_index(topi[:, t, :], top[:, t, :], logit[:, t, :]), b)
                dve.tensor_copy(topf[:, two, :], topi[:, two, 0:2]).then_inc(v_chain, 1)
                chain[0] += 1
                dve.tensor_tensor(gap[:, two], top[:, two, 1], top[:, two, 0], ALU.subtract).then_inc(gap_ready, 1)

            def router_end(b):
                two = slice(2 * b, 2 * b + 2)
                dve.wait_ge(e2_ready, b + 1)
                link(dve.tensor_scalar(den[:, two], e2[:, two], 1.0, None, ALU.add))
                link(dve.reciprocal(gw[:, two, 0], den[:, two]))
                link(dve.tensor_tensor(gw[:, two, 1], e2[:, two], gw[:, two, 0], ALU.mult))

            def router_weights(b):
                two = slice(2 * b, 2 * b + 2)
                for t in range(2 * b, 2 * b + 2):
                    dve.tensor_scalar(hot[:, t, :], rw("iota"), topf[:, t, 0:1], gw[:, t, 0:1],
                                      ALU.is_equal, ALU.mult).then_inc(v_chain, 1)
                    chain[0] += 1
                both(lambda t: dve.tensor_scalar(comb[:, t, 0:E], rw("iota"), topf[:, t, 1:2], gw[:, t, 1:2],
                                                 ALU.is_equal, ALU.mult), b)
                ins = dve.tensor_tensor(comb[:, two, 0:E], comb[:, two, 0:E], hot[:, two, :], ALU.add)
                ins.then_inc(comb_ready, 1)
                dve.wait_ge(comb_ready, b + 1)

            def acc_bias(b):
                dve.wait_ge(turn_full, full(f"b2{b}"))
                dve.wait_ge(acc_done, acc_no[0])
                dve.tensor_tensor(acc[:, b, :], turn[:, 0:S], acc[:, b, :], ALU.add).then_inc(turn_free, 1)
                dve.wait_ge(turn_free, full(f"b2{b}"))
                dve.engine_nop().then_inc(acc_done, 1)
                acc_no[0] += 1

            acc_no = [0]

            def accumulate(n):
                b, o = n // EX, n % EX
                dve.wait_ge(down_done, HC * (n + 1))
                src = bank[4 + n % 3][:, 0:S]
                if o == 0:
                    dve.tensor_tensor(acc[:, b, :], src, x2_t[:, b, :], ALU.add).then_inc(mul_done, 1)
                else:
                    if o % 2:
                        dve.wait_ge(cb_ready[o // 2], 16 * (b + 1))
                    if acc_no[0]:
                        dve.wait_ge(acc_done, acc_no[0])
                    dve.tensor_tensor(tmp[:, :], src, cb[:, b, order[o], :], ALU.mult).then_inc(mul_done, 1)

            def accumulate_end(n):
                b, o = n // EX, n % EX
                dve.wait_ge(mul_done, n + 1)
                if o == 0:
                    return
                dve.wait_ge(acc_done, acc_no[0])
                dve.tensor_tensor(acc[:, b, :], tmp[:, :], acc[:, b, :], ALU.add).then_inc(acc_done, 1)
                acc_no[0] += 1

            def unit_parts(u):
                if u >= 4:
                    dve.wait_ge(down_done, u - 3)
                if u % 2 == 0:
                    dve.wait_ge(gelu_done, u + 1)
                    dve.tensor_copy(h_high[:, u % 4, :], hs(u)).then_inc(high_by_v, 1)
                else:
                    dve.wait_ge(high_by_a, u // 2 + 1)
                    dve.tensor_tensor(h_low[:, u % 4, :], hs(u), h_high[:, u % 4, :].bitcast(F32),
                                      ALU.subtract).then_inc(low_by_v, 1)

            def last_norm(b):
                dve.wait_ge(turn_full, full(f"fin{b}"))
                norm(5 + b, b, fin, fin_ready, turn[:, 0:S].rearrange("p (q n) -> p q n", q=QT))

            def last_norm_end(b):
                norm_end(5 + b, b, fin, fin_ready, turn[:, 0:S].rearrange("p (q n) -> p q n", q=QT))
                dve.wait_ge(fin_ready, b + 1)
                dve.engine_nop().then_inc(turn_free, 1)

            dve.wait_ge(mbias_ready, QT)
            for g in range(GH):
                row_max(0, g)
            neg_max(0)
            take_negmax(0)
            for i in range(STEPS):
                for g in range(GH):
                    if i + 1 < STEPS:
                        row_max(i + 1, g)
                    what = inside.get((i, g - 1), "")
                    if (i, g) == (1, 0):
                        dve.wait_ge(v_taken, 2)
                        dve.memset(bank[6][:, 0:S], 0.0).then_inc(pv_zero, 1)
                    if what == "out_w1":
                        residual(1)
                        dve.wait_ge(turn_free, full("out_w1"))
                        norm(2, 1, x1, x1_ready)
                    if (i, g) == (1, 0):
                        norm_end(2, 1, x1, x1_ready)
                    if what == "q1":
                        split_q(1)
                    if what.startswith("o") and what[1:].isdigit():
                        take_out(int(what[1:]))
                    if what == "wo0":
                        after_attention(0)
                    if (i, g) == (7, 0):
                        norm_end(3, 0, x2, x2_ready)
                    if what == "gate0":
                        x2_low(0)
                        router(0)
                if inside.get((i, GH - 1)) == "o4":
                    take_out(4)
                if i + 1 < STEPS:
                    neg_max(i + 1)
                    take_negmax(i + 1)
            take_out(6)
            router_end(0)
            router_weights(0)
            for u in range(UNITS):
                unit_parts(u)
                what = taken.get(u)
                if what == "o7":
                    take_out(7)
                if what == "wo1":
                    after_attention(1)
                if u == at["wo1"] + 3:
                    norm_end(4, 1, x2, x2_ready)
                if what in ("b20", "b21"):
                    acc_bias(int(what[-1]))
                if what == "gate1":
                    x2_low(1)
                    router(1)
                if u == at["gate1"] + 2:
                    router_end(1)
                if u == at["gate1"] + 3:
                    router_weights(1)
                if what == "fin0":
                    last_norm(0)
                if u == at["fin0"] + 2:
                    last_norm_end(0)
                if u % HC == LAG % HC and u >= HC + LAG:
                    accumulate((u - HC - LAG) // HC)
                if u % HC == (LAG + 1) % HC and u >= HC + LAG + 1:
                    accumulate_end((u - HC - LAG - 1) // HC)
            done = (UNITS - HC - LAG - 1) // HC
            for n in range(done + (0 if (UNITS - 1) % HC == LAG % HC else 1), B * EX):
                accumulate(n)
                accumulate_end(n)
            last_norm(1)
            last_norm_end(1)


_OUT = ((B, S, P), "float32")


def kernel(**inputs):
    import numpy as np
    import concourse.bacc as bacc
    from concourse.bass_utils import run_bass_kernel_spmd

    def a(name):
        return np.asarray(inputs[name])

    x, c = a("x"), a("ctx_1024")
    w = a("L0_attn_in_proj_weight").T
    arrays = {
        "x_t_w": np.concatenate([w[:, 0:2 * P], w[:, P:3 * P], x.reshape(B * S, P).T], axis=1),
        "x_tok": x.reshape(NT, P, P).transpose(1, 0, 2),
        "ctx_w": np.concatenate([c.reshape(B * SK, P).T, a("L0_xattn_wk").T, a("L0_xattn_wv").T], axis=1),
        "cols": np.concatenate([
            np.eye(P, dtype=np.float32), a("L0_attn_out_w").T, a("L0_xattn_wq").T, a("L0_xattn_wo").T,
            a("L0_ffn_gate_w"), a("L0_ffn_b1").reshape(E * HC, P).T, a("L0_ffn_bs1").reshape(HC, P).T,
            a("L0_xattn_bk").reshape(P, 1)], axis=1),
        "rows": np.concatenate([
            a("L0_attn_in_proj_bias"), a("L0_attn_rel_pos_keys")[REL - 1:REL + 2, 0:D].reshape(-1),
            a("L0_attn_out_b"), a("L0_xattn_bq"), a("L0_xattn_bv"), a("L0_xattn_bo"), a("L0_ffn_gate_b"),
            np.arange(E, dtype=np.float32), np.full(4, np.e, np.float32), np.full(4, -0.5, np.float32)])[None, :],
        "b2_rows": np.concatenate([a("L0_ffn_b2"), a("L0_ffn_bs2")[None, :]], axis=0),
        "mask": a("mask_1x1xSxS2_ik0").reshape(QT, P, SK).transpose(1, 0, 2),
        "w1": np.concatenate([a("L0_ffn_w1"), a("L0_ffn_ws1")[None]], axis=0).transpose(1, 0, 2),
        "w2": np.concatenate([a("L0_ffn_w2"), a("L0_ffn_ws2")[None]], axis=0)
              .reshape(EX, HC, P, P).transpose(2, 0, 1, 3),
    }
    arrays = {k: np.ascontiguousarray(v) for k, v in arrays.items()}
    nc = bacc.Bacc("TRN2", target_bir_lowering=False, num_devices=1)
    aps = {k: nc.dram_tensor(k, v.shape, mybir.dt.from_np(v.dtype), kind="ExternalInput").ap()
           for k, v in arrays.items()}
    aps["rows"] = aps["rows"].broadcast_to([P, ROW_N])
    y = nc.dram_tensor("y", _OUT[0], F32, kind="ExternalOutput").ap()
    heads = nc.dram_tensor("heads", (H, D, 3, B * SK), F32, kind="Internal").ap()
    weights = nc.dram_tensor("weights", (B, E, S), F32, kind="Internal").ap()
    decoder_layer(nc, *aps.values(), heads, weights, y)
    r = run_bass_kernel_spmd(nc, [arrays], core_ids=[0])
    return r.results[0]["y"]
```
